# Optimizing a Trainium2 kernel written in Bass

```python
import numpy as np
import jax
import jax.numpy as jnp

def _softmax(x, axis=-1):
    return jax.nn.softmax(x, axis=axis)

def _gelu(x):
    return jax.nn.gelu(x, approximate=True)

def _silu(x):
    return jax.nn.silu(x)

def _sigmoid(x):
    return jax.nn.sigmoid(x)

def _layernorm(x, axis=-1, eps=1e-05):
    m = jnp.mean(x, axis=axis, keepdims=True)
    v = jnp.var(x, axis=axis, keepdims=True)
    return (x - m) / jnp.sqrt(v + eps)

def _scatter_add(tgt, idx, src, axis=0):
    return tgt.at[idx].add(src)

def _segment_sum(src, seg, n):
    return jax.ops.segment_sum(src, seg, n)
kernel_name = 'mk_prb_d1_jaxref_r8_1df775'

def setup_inputs(seed: int=0):
    np.random.seed(seed)
    _w = jnp.asarray

    def _L0_attn_setup():
        import jax, jax.numpy as jnp
        import numpy as np
        B, T, D, H = (4, 256, 128, 16)
        HD = D // H
        EPS = 1e-05
        NEG = 10000000000.0
        key = jax.random.key(seed)
        k1, k2, k3 = jax.random.split(key, 3)
        return {'target': jax.random.normal(k1, (B, T, D), dtype=jnp.float32), 'w_qkv': jax.random.normal(k2, (D, 3 * D), dtype=jnp.float32) * 0.02, 'w_proj': jax.random.normal(k3, (D, D), dtype=jnp.float32) * (0.02 / np.sqrt(24.0)), 'b_proj': jnp.zeros((D,), dtype=jnp.float32), 'ln_gamma': jnp.ones((D,), dtype=jnp.float32), 'ln_beta': jnp.zeros((D,), dtype=jnp.float32)}
    _L0_attn_in = _L0_attn_setup()

    def _L0_ffn_setup():
        import jax, jax.numpy as jnp
        import numpy as np
        E, D, MULT, K = (8, 128, 4, 2)
        B, S = (4, 256)
        H = MULT * D
        key = jax.random.key(seed)
        k0, k1, k2, k3 = jax.random.split(key, 4)
        x = jax.random.normal(k0, (B, S, D), dtype=jnp.float32)
        Wr = jax.random.normal(k1, (E, D), dtype=jnp.float32) * D ** (-0.5)
        W1 = jax.random.normal(k2, (E, D, H), dtype=jnp.float32) * D ** (-0.5)
        b1 = jnp.zeros((E, H), dtype=jnp.float32)
        W2 = jax.random.normal(k3, (E, H, D), dtype=jnp.float32) * H ** (-0.5)
        b2 = jnp.zeros((E, D), dtype=jnp.float32)
        return {'x': x, 'Wr': Wr, 'W1': W1, 'b1': b1, 'W2': W2, 'b2': b2}
    _L0_ffn_in = _L0_ffn_setup()
    _d = {'L0_attn_target': _L0_attn_in['target'], 'L0_attn_w_qkv': _L0_attn_in['w_qkv'], 'L0_attn_w_proj': _L0_attn_in['w_proj'], 'L0_attn_b_proj': _L0_attn_in['b_proj'], 'L0_attn_ln_gamma': _L0_attn_in['ln_gamma'], 'L0_attn_ln_beta': _L0_attn_in['ln_beta'], 'L0_ffn_Wr': _L0_ffn_in['Wr'], 'L0_ffn_W1': _L0_ffn_in['W1'], 'L0_ffn_b1': _L0_ffn_in['b1'], 'L0_ffn_W2': _L0_ffn_in['W2'], 'L0_ffn_b2': _L0_ffn_in['b2']}
    _x0 = _d['L0_attn_target']
    _d['L0_attn_target'] = jax.random.normal(jax.random.fold_in(jax.random.key(seed), 1), (32, 256, 128), dtype=_x0.dtype)
    del _x0
    return _d

def reference(L0_attn_target, L0_attn_w_qkv, L0_attn_w_proj, L0_attn_b_proj, L0_attn_ln_gamma, L0_attn_ln_beta, L0_ffn_Wr, L0_ffn_W1, L0_ffn_b1, L0_ffn_W2, L0_ffn_b2):

    def _L0_attn_ref(target, w_qkv, w_proj, b_proj, ln_gamma, ln_beta):
        import jax, jax.numpy as jnp
        import numpy as np
        B, T, D, H = (4, 256, 128, 16)
        HD = D // H
        EPS = 1e-05
        NEG = 10000000000.0
        b, t, d = target.shape
        resid = target
        qkv = target @ w_qkv
        q, k, v = jnp.split(qkv, 3, axis=-1)
        q = q.reshape(b, t, H, HD).transpose(0, 2, 1, 3)
        k = k.reshape(b, t, H, HD).transpose(0, 2, 1, 3)
        v = v.reshape(b, t, H, HD).transpose(0, 2, 1, 3)
        scores = jnp.einsum('bhqd,bhkd->bhqk', q, k) * (1.0 / np.sqrt(HD))
        causal = (jnp.arange(t)[:, None] >= jnp.arange(t)[None, :]).astype(scores.dtype)
        scores = scores * causal - (1.0 - causal) * NEG
        attn = jax.nn.softmax(scores, axis=-1)
        out = jnp.einsum('bhqk,bhkd->bhqd', attn, v)
        out = out.transpose(0, 2, 1, 3).reshape(b, t, d)
        proj = out @ w_proj + b_proj
        x = proj + resid
        mu = jnp.mean(x, axis=-1, keepdims=True)
        var = jnp.var(x, axis=-1, keepdims=True)
        return (x - mu) * jax.lax.rsqrt(var + EPS) * ln_gamma + ln_beta

    def _L0_ffn_ref(x, Wr, W1, b1, W2, b2):
        import jax, jax.numpy as jnp
        import numpy as np
        E, D, MULT, K = (8, 128, 4, 2)
        B, S = (4, 256)
        H = MULT * D
        probs = jax.nn.softmax(jnp.einsum('bsd,ed->bse', x, Wr), axis=-1)
        topv, topi = jax.lax.top_k(probs, K)
        combine = jnp.sum(topv[..., None] * jax.nn.one_hot(topi, E, dtype=x.dtype), axis=2)

        def body(acc, params):
            w1, bb1, w2, bb2, ce = params
            h = jax.nn.gelu(jnp.einsum('bsd,dh->bsh', x, w1) + bb1, approximate=False)
            y = jnp.einsum('bsh,hd->bsd', h, w2) + bb2
            return (acc + ce[..., None] * y, None)
        cE = jnp.moveaxis(combine, -1, 0)
        out, _ = jax.lax.scan(body, jnp.zeros_like(x), (W1, b1, W2, b2, cE))
        return out
    x = L0_attn_target
    xn = _layernorm(x, axis=-1)
    x = x + _L0_attn_ref(xn, L0_attn_w_qkv, L0_attn_w_proj, L0_attn_b_proj, L0_attn_ln_gamma, L0_attn_ln_beta) + _L0_ffn_ref(xn, L0_ffn_Wr, L0_ffn_W1, L0_ffn_b1, L0_ffn_W2, L0_ffn_b2)
    return x

_drawn_inputs = setup_inputs


def setup_inputs(seed=0):
    import zlib

    import numpy as np

    out = dict(_drawn_inputs(seed))
    spreads = {'L0_attn_b_proj': (0.0, 0.1),
     'L0_attn_ln_gamma': (1.0, 0.2),
     'L0_attn_ln_beta': (0.0, 0.1),
     'L0_ffn_b1': (0.0, 0.544),
     'L0_ffn_b2': (0.0, 0.371)}
    factors = {'L0_attn_w_qkv': 8.0, 'L0_attn_w_proj': 8.0}
    for name, (base, spread) in spreads.items():
        noise = np.random.default_rng([zlib.crc32(name.encode()), seed]).standard_normal(out[name].shape)
        drawn = base * np.exp(spread * noise) if base else spread * noise
        out[name] = jnp.asarray(drawn.astype(out[name].dtype))
    for name, factor in factors.items():
        out[name] = (out[name] * factor).astype(out[name].dtype)
    return out
```

```python
from contextlib import ExitStack

import concourse.bass as bass
from concourse import mybir

F32 = mybir.dt.float32
F16 = mybir.dt.float16
BF16 = mybir.dt.bfloat16
I32 = mybir.dt.int32
U32 = mybir.dt.uint32
ALU = mybir.AluOpType
ACT = mybir.ActivationFunctionType
AX = mybir.AxisListType

P = 128


def attention_and_moe(nc, x, w_qkv, w_proj, b_proj, gamma, beta, w_router, w1, b1, w2, b2, out):
    B, T, D = x.shape
    E, _, HID = w1.shape
    H = 16
    HD = D // H
    QT = T // P
    NT = B * QT
    HC = HID // P
    G, J = 4, 4
    ROWS = P // J
    LN_EPS = 1e-5
    SCALE = 1.0 / HD ** 0.5
    SHIFT_UNIT = 64.0
    MASKED = 32768.0
    S = 2 * P
    NS = B * T * 2 // S + E
    assert D == P and QT == 2 and HD == 8 and G * J == H

    ctx = ExitStack()
    with ctx:
        def sb(name, shape, dt=F32):
            return ctx.enter_context(nc.sbuf_tensor(name, shape, dt))

        def sem(name):
            return ctx.enter_context(nc.semaphore(name))

        x_all = sb("x_all", [P, NT, D])
        xn_all = sb("xn_all", [P, NT, D])
        ident = sb("ident", [P, P])
        ident16 = sb("ident16", [P, P], F16)
        mask16 = sb("mask16", [P, P], F16)
        wqkv = sb("wqkv", [P, 3 * D])
        wq_rep = sb("wq_rep", [P, G, P])
        wk_rep = sb("wk_rep", [P, G, P])
        wp = sb("wp", [P, D])
        wr = sb("wr", [E, D])
        wrT = sb("wrT", [P, E])
        bproj_bc = sb("bproj_bc", [P, D])
        gamma_bc = sb("gamma_bc", [P, D])
        beta_bc = sb("beta_bc", [P, D])
        row_id = sb("row_id", [P, ROWS])
        row_col = sb("row_col", [P, 1])
        q_low = sb("q_low", [P, 1])
        k_low = sb("k_low", [P, 1])
        k_one = sb("k_one", [P, 1])
        stats = sb("stats", [P, NT, 6])
        mean = sb("mean", [P, NT])
        var = sb("var", [P, NT])
        dev = sb("dev", [P, NT])
        rstd = sb("rstd", [P, NT])
        half = sb("half", [P, NT])
        stage = sb("stage", [P, 2, 4, D])
        stage_T = sb("stage_T", [P, 2, 4 * P])
        logits = sb("logits", [P, NT, E])

        xb = sb("xb", [P, 2, QT, D])
        xbT = sb("xbT", [P, 2, T])
        q_hi = sb("q_hi", [P, G * T], F16)
        k_hi = sb("k_hi", [P, G * T], F16)
        q_cat = sb("q_cat", [P, G, T], F16)
        k_cat = sb("k_cat", [P, 2, G, T], F16)
        q_diag = sb("q_diag", [P, 2, G, J, T], F16)
        v_aug = sb("v_aug", [P, 2, QT, H, 32])
        shift = sb("shift", [P, QT, J, G])
        shift_T = sb("shift_T", [H, 2, T], F16)
        probs = sb("probs", [P, 6, 2 * 512])
        o_T = sb("o_T", [P, G, T])
        rden = sb("rden", [P, H])
        o_n = sb("o_n", [P, QT, H, HD])
        o_nT = sb("o_nT", [P, T])
        xpb = sb("xpb", [P, QT, D])
        x2 = sb("x2", [P, QT, D])
        st2 = sb("st2", [P, QT, 6])
        mv2 = sb("mv2", [P, QT, 2])
        rstd2 = sb("rstd2", [P, QT])
        y2 = sb("y2", [P, QT, D])
        res = sb("res", [P, QT, D])

        prob = sb("prob", [P, NT, E])
        prob2, key, total, rank = (probs[:, u, 0:NT * E].rearrange("p (t e) -> p t e", e=E) for u in range(4))
        past = probs[:, 4, 0:NS * E].rearrange("p (t e) -> p t e", e=E)
        pick = sb("pick", [P, 2, NT, E])
        picked16 = sb("picked16", [P, NT, E], BF16)
        top = sb("top", [P, 2, NT])
        red = sb("red", [P, NT])
        order = sb("order", [P, E])
        before16 = sb("before16", [P, P], BF16)
        ones16 = sb("ones16", [P, P], BF16)
        ones = sb("ones", [P, NT])
        padded = sb("padded", [P, E])
        padded_i = sb("padded_i", [P, E], I32)
        ends = sb("ends", [P, E])
        tile_start = sb("tile_start", [P, NS])
        expert = sb("expert", [P, NS])
        expert_i = sb("expert_i", [P, NS], I32)
        slot = sb("slot", [P, 2, NT])
        slot_i = sb("slot_i", [P, NT, 2], U32)
        zeros = sb("zeros", [P, NS * S // P // 16 * D])
        send = sb("send", [P, 4, D])
        send_i = sb("send_i", [P, 4, 2], U32)
        w2_all = sb("w2_all", [P, E, HC, D])
        b1_all = sb("b1_all", [P, E, HC])
        b2_bc = sb("b2_bc", [P, E, D])
        xg = sb("xg", [P, 2, 2, D])
        xgT = sb("xgT", [P, 2, S])
        w1b = sb("w1b", [P, 2, HID])
        hT = probs[:, 0:4, :].rearrange("p (b c) (x s) -> p b (c x) s", b=2, s=S)
        y = sb("y", [P, 2, 2, D])
        back_i = sb("back_i", [P, 4, 2], U32)
        got = xn_all[:, 0:8, :].rearrange("p (u c) d -> p u c d", c=2)
        fin = xn_all[:, 8:12, :]

        x_slots = nc.dram_tensor("x_slots", [NS * S, D], F32).ap()
        y_slots = nc.dram_tensor("y_slots", [NS * S, D], F32).ap()

        wide = [ctx.enter_context(nc.psum_tensor(f"wide{i}", [P, 1024], F32)) for i in range(2)]
        bank = {n: ctx.enter_context(nc.psum_tensor(f"bank_{n}", [P, 512], F32)) for n in ("maxA", "maxB", "head", "misc")}

        x_loaded = [sem(f"x_loaded{c}") for c in range(4)]
        weights_loaded = sem("weights_loaded")
        consts = sem("consts")
        prep = sem("prep")
        prep_act = sem("prep_act")
        var_ready = sem("var_ready")
        rstd_ready = sem("rstd_ready")
        staged = sem("staged")
        stage_copied = sem("stage_copied")
        stage_T_filled = sem("stage_T_filled")
        stage_T_ready = sem("stage_T_ready")
        stage_T_used = sem("stage_T_used")
        wrT_filled = sem("wrT_filled")
        wrT_ready = sem("wrT_ready")
        logits_filled = sem("logits_filled")

        filled = {n: sem(f"filled_{n}") for n in ("wide0", "wide1", "maxA", "maxB", "head", "misc")}
        drained = {n: sem(f"drained_{n}") for n in filled}
        xb_ready = sem("xb_ready")
        xbT_ready = sem("xbT_ready")
        hi_ready = sem("hi_ready")
        q_cat_ready = sem("q_cat_ready")
        k_cat_ready = sem("k_cat_ready")
        q_diag_loaded = sem("q_diag_loaded")
        v_ready = sem("v_ready")
        shift_hi_ready = sem("shift_hi_ready")
        shift_ready = sem("shift_ready")
        shift_T_ready = sem("shift_T_ready")
        shift_loaded = sem("shift_loaded")
        exp_ready = sem("exp_ready")
        probs_ready = sem("probs_ready")
        o_T_ready = sem("o_T_ready")
        rden_ready = sem("rden_ready")
        o_n_ready = sem("o_n_ready")
        o_nT_ready = sem("o_nT_ready")
        xpb_ready = sem("xpb_ready")
        x2_ready = sem("x2_ready")
        st2_ready = sem("st2_ready")
        mv2_ready = sem("mv2_ready")
        rstd2_ready = sem("rstd2_ready")
        y2_ready = sem("y2_ready")
        res_steps = sem("res_steps")
        tile_done = sem("tile_done")
        stored = [sem(f"stored{u}") for u in range(4)]
        expert_weights = sem("expert_weights")
        zeros_ready = sem("zeros_ready")
        slots_zeroed = sem("slots_zeroed")
        exp_router = sem("exp_router")
        route = sem("route")
        route_counts = sem("route_counts")
        send_ready = sem("send_ready")
        sent = [sem(f"sent{u}") for u in range(4)]
        xg_loaded = [sem(f"xg_loaded{u}") for u in range(2)]
        w1_loaded = [sem(f"w1_loaded{u}") for u in range(2)]
        xg_T_filled = sem("xg_T_filled")
        xg_T_ready = sem("xg_T_ready")
        h_filled = sem("h_filled")
        h_ready = sem("h_ready")
        y_filled = sem("y_filled")
        y_ready = sem("y_ready")
        y_stored = [sem(f"y_stored{u}") for u in range(2)]
        got_ready = [sem(f"got_ready{u}") for u in range(4)]
        back_ready = sem("back_ready")
        fin_step = sem("fin_step")
        fin_ready = sem("fin_ready")
        attention_done = sem("attention_done")

        FRONT, BACK = "front", "back"
        USES = [
            ("misc", "xT", FRONT),
            ("wide0", "s0", BACK), ("wide1", "s1", BACK),
            ("wide0", "q", FRONT), ("wide1", "k", FRONT), ("misc", "v", FRONT),
            ("wide0", "s2", BACK), ("wide1", "s3", BACK),
            *[(("maxA", "maxB")[u % 2], f"m{u}", FRONT) for u in range(0, 3)],
            ("head", "o0", BACK),
            ("wide0", "s4", BACK),
            *[(("maxA", "maxB")[u % 2], f"m{u}", FRONT) for u in range(3, 6)],
            ("wide1", "s5", BACK),
            *[(("maxA", "maxB")[u % 2], f"m{u}", FRONT) for u in range(6, 9)],
            ("head", "o1", BACK),
            *[(("maxA", "maxB")[u % 2], f"m{u}", FRONT) for u in range(9, 12)],
            ("misc", "oT0", BACK), ("misc", "oT1", BACK),
            ("misc", "shift", FRONT),
            ("head", "onT", BACK), ("head", "proj", BACK),
        ]
        SCORES = [(0, (0,)), (0, (1,)), (1, (0, 1)), (0, (2,)), (0, (3,)), (1, (2, 3))]

        def halves(s):
            if isinstance(s, int):
                return ([FRONT] if s < B else []) + ([BACK] if s > 0 else [])
            return [FRONT, BACK]

        def use(s, what):
            name = next(n for n, w, _ in USES if w == what)
            mine = [(w, h) for n, w, h in USES if n == name]
            done = {h: sum(x == h for _, x in mine) for h in (FRONT, BACK)}
            at = [w for w, h in mine if h in halves(s)].index(what)
            if isinstance(s, int):
                before = s * done[FRONT] + max(s - 1, 0) * done[BACK] + at
            else:
                before = s * (done[FRONT] + done[BACK]) + (at - done[BACK])
            return name, before

        def buf(name):
            return wide[int(name[-1])] if name.startswith("wide") else bank[name]

        def wait_room(eng, s, what):
            name, before = use(s, what)
            if not isinstance(before, int) or before > 0:
                eng.wait_ge(drained[name], before)
            return buf(name), filled[name]

        def wait_full(eng, s, what):
            name, before = use(s, what)
            eng.wait_ge(filled[name], before + 1)
            return buf(name), drained[name]

        def steps(eng, step):
            step(0, 0)
            with eng.Fori(0, (B - 2) // 2) as i:
                for k in range(2):
                    step(i * 2 + (1 + k), (1 + k) % 2)
            step(B - 1, (B - 1) % 2)
            step(B, B % 2)

        def tiles(eng, step):
            for s in range(4):
                step(s, s % 2)
            with eng.Fori(0, (NS - 4) // 2) as i:
                for k in range(2):
                    step(i * 2 + (4 + k), k)
            step(NS, 0)
            step(NS + 1, 1)

        def rounds(eng, body):
            body(0)
            with eng.Fori(1, NT // 4) as i:
                body(i)

        def is_later(i):
            return not isinstance(i, int) or i > 0

        def first(s):
            return s < NS if isinstance(s, int) else True

        def second(s):
            return s >= 2 if isinstance(s, int) else True

        def later(eng, sem_, count, when):
            if when:
                eng.wait_ge(sem_, count)

        LOOP2 = NT // 8

        ROUTE_PICKED = 17
        ROUTE_DONE = 43

        block = ctx.enter_context(nc.Block())

        @block.sync
        def _(sp):
            xt = x.rearrange("b (t p) d -> p (b t) d", p=P)
            n = NT // 4
            for c in range(4):
                sp.dma_start(x_all[:, c * n:(c + 1) * n, :], xt[:, c * n:(c + 1) * n, :]).then_inc(x_loaded[c], 16)

            sp.wait_ge(zeros_ready, 1)
            xs = x_slots.rearrange("(c p r) d -> c p (r d)", c=16, p=P)
            for c in range(16):
                sp.dma_start(xs[c, :, :], zeros[:, :]).then_inc(slots_zeroed, 16)
            sp.dma_start(w2_all[:, :, :, :], w2.rearrange("e (c p) d -> p e c d", p=P)).then_inc(expert_weights, 16)
            with nc.allow_non_contiguous_dma(reason="biases by hidden unit, once"):
                sp.dma_start(b1_all[:, :, :], b1.rearrange("e (c p) -> p e c", p=P)).then_inc(expert_weights, 16)
            sp.dma_start(b2_bc[:, :, :], b2.rearrange("(o e) d -> o e d", o=1).to_broadcast([P, E, D])).then_inc(expert_weights, 16)

            def step(s, par):
                if FRONT in halves(s):
                    sp.wait_ge(q_cat_ready, s + 1)
                    for j in range(J):
                        rows = slice(ROWS * j, ROWS * (j + 1))
                        sp.dma_start(q_diag[rows, par, :, j, :], q_cat[rows, :, :]).then_inc(q_diag_loaded, 16)
                    sp.wait_ge(shift_T_ready, s + 1)
                    sp.nop(nofuse=True)
                    sp.wait_ge(q_diag_loaded, (s + 1) * (16 * J))
                    sp.nop(nofuse=True)
                    for j in range(J):
                        for part in range(2):
                            row = ROWS * j + 3 * HD + part
                            sp.dma_start(q_diag[row:row + 1, par, :, j, :],
                                         shift_T[G * j:G * (j + 1), part, :]).then_inc(shift_loaded, 16)

            steps(sp, step)

            sp.wait_ge(route, ROUTE_DONE)
            for u in range(4):
                sp.wait_ge(sent[u], 32 * (NT // 4))

            def tile(s, par):
                if not first(s):
                    return
                e = sp.value_load(expert_i[0:1, bass.ds(s, 1)], min_val=0, max_val=E - 1)
                later(sp, xg_T_filled, s - 1, second(s))
                sp.nop(nofuse=True)
                sp.dma_start(xg[:, par, :, :], x_slots[bass.ds(s * S, S), :].rearrange("(t p) d -> p t d", p=P)).then_inc(xg_loaded[par], 16)
                later(sp, h_filled, s - 1, second(s))
                sp.nop(nofuse=True)
                sp.dma_start(w1b[:, par, :], w1[bass.ds(e, 1), :, :].rearrange("o p h -> (o p) h")).then_inc(w1_loaded[par], 16)

            tiles(sp, tile)
            ot = out.rearrange("b (t p) d -> (b t) p d", p=P)
            with sp.Fori(0, NT // 4) as i:
                for u in range(4):
                    sp.wait_ge(fin_ready, i * 4 + (u + 1))
                    sp.nop(nofuse=True)
                    sp.dma_start(ot[bass.ds(i * 4 + u, 1), :, :].rearrange("o p d -> (o p) d"), fin[:, u, :]).then_inc(stored[u], 16)
            for u in range(4):
                sp.wait_ge(stored[u], 16 * (NT // 4 + 1))

        @block.gpsimd
        def _(pool):
            pool.memset(zeros[:, :], 0.0).then_inc(zeros_ready, 1)
            pool.memset(ident[:, :], 0.0).then_inc(consts, 1)
            pool.memset(ident16[:, :], 0.0).then_inc(consts, 1)
            pool.memset(mask16[:, :], 0.0).then_inc(consts, 1)
            pool.memset(half[:, :], -0.5).then_inc(consts, 1)
            pool.memset(q_diag[:, :, :, :, :], 0.0).then_inc(consts, 1)
            pool.memset(v_aug[:, :, :, :, :], 0.0).then_inc(consts, 1)
            pool.memset(wq_rep[:, :, :], 0.0).then_inc(consts, 1)
            pool.memset(wk_rep[:, :, :], 0.0).then_inc(consts, 1)
            pool.iota(row_col[:, :], pattern=[[0, 1]], base=0, channel_multiplier=1,
                      allow_small_or_imprecise_dtypes=True).then_inc(consts, 1)
            pool.iota(order[:, :], pattern=[[-1, E]], base=E, channel_multiplier=0,
                      allow_small_or_imprecise_dtypes=True).then_inc(consts, 1)
            pool.iota(tile_start[:, :], pattern=[[S, NS]], base=0, channel_multiplier=0,
                      allow_small_or_imprecise_dtypes=True).then_inc(consts, 1)
            pool.memset(ones[:, :], 1.0).then_inc(consts, 1)
            pool.memset(ones16[:, :], 1.0).then_inc(consts, 1)
            pool.memset(before16[:, :], 1.0).then_inc(consts, 1)
            pool.wait_ge(consts, 14)
            pool.affine_select(out=before16[:, :], in_=before16[:, :], compare_op=ALU.is_gt, fill=0.0, base=0,
                               pattern=[[1, P]], channel_multiplier=-1).then_inc(consts, 1)
            pool.memset(v_aug[:, :, :, :, HD:HD + 1], 1.0).then_inc(consts, 1)
            pool.affine_select(out=ident[:, :], in_=ident[:, :], compare_op=ALU.not_equal, fill=1.0, base=0,
                               pattern=[[-1, P]], channel_multiplier=1).then_inc(consts, 1)
            pool.affine_select(out=ident16[:, :], in_=ident16[:, :], compare_op=ALU.not_equal, fill=MASKED, base=0,
                               pattern=[[-1, P]], channel_multiplier=1).then_inc(consts, 1)
            pool.affine_select(out=mask16[:, :], in_=mask16[:, :], compare_op=ALU.is_ge, fill=-MASKED, base=0,
                               pattern=[[-1, P]], channel_multiplier=1).then_inc(consts, 1)
            pool.wait_ge(var_ready, 1)
            pool.tensor_tensor(rstd[:, :], var[:, :], half[:, :], ALU.pow).then_inc(rstd_ready, 1)
            with pool.Fori(0, LOOP2) as i:
                for k in range(2):
                    pool.wait_ge(staged, i * 2 + (k + 1))
                    pool.tensor_copy(xn_all[:, bass.ds(i * 8 + 4 * k, 4), :], stage[:, k, :, :]).then_inc(stage_copied, 1)

            pool.wait_ge(stage_copied, 2 * LOOP2)
            pool.wait_ge(route, ROUTE_DONE)
            pool.wait_ge(slots_zeroed, 256)

            def send_round(i):
                for u in range(4):
                    t = i * 4 + u
                    later(pool, sent[u], i * 32, is_later(i))
                    pool.tensor_copy(send[:, u, :], xn_all[:, bass.ds(t, 1), :].rearrange("p a d -> p (a d)")).then_inc(send_ready, 1)
                    pool.tensor_copy(send_i[:, u, :], slot_i[:, bass.ds(t, 1), :].rearrange("p a d -> p (a d)")).then_inc(send_ready, 1)
                    pool.wait_ge(send_ready, i * 8 + (2 * u + 2))
                    pool.nop(nofuse=True)
                    for c in range(2):
                        pool.indirect_dma_start(out=x_slots, out_offset=bass.IndirectOffsetOnAxis(ap=send_i[:, u, c:c + 1], axis=0),
                                                in_=send[:, u, :], in_offset=None).then_inc(sent[u], 16)

            rounds(pool, send_round)

            def copy_in(s, par):
                pool.tensor_copy(xb[:, par, :, :], xn_all[:, bass.ds(s * QT, QT), :]).then_inc(xb_ready, 1)

            copy_in(0, 0)
            copy_in(1, 1)

            def step(s, par):
                if BACK not in halves(s):
                    return
                b = s - 1
                if not (isinstance(b, int) and b == 0):
                    pool.wait_ge(x2_ready, b * 1)
                pool.tensor_tensor(xpb[:, 0, :], xn_all[:, bass.ds(b * QT, 1), :].rearrange("p a d -> p (a d)"), bproj_bc[:, :], ALU.add).then_inc(xpb_ready, 1)
                pool.tensor_tensor(xpb[:, 1, :], xn_all[:, bass.ds(b * QT + 1, 1), :].rearrange("p a d -> p (a d)"), bproj_bc[:, :], ALU.add).then_inc(xpb_ready, 1)
                for u, (kt, gs) in enumerate(SCORES):
                    pool.wait_ge(exp_ready, b * 6 + (u + 1))
                    pool.nop(nofuse=True)
                    n, width = (J, T) if kt == 0 else (2 * J, P)
                    part = probs[:, u, :].rearrange("p (j q) -> p j q", q=width)[:, :, 0:P]
                    pool.affine_select(out=part, in_=part, compare_op=ALU.is_ge, fill=0.0, base=0,
                                       pattern=[[0, n], [1, P]], channel_multiplier=-1).then_inc(probs_ready, 1)
                if not isinstance(s, int) or s + 1 < B:
                    copy_in(s + 1, 1 - par)
                pool.wait_ge(mv2_ready, b * 3 + 3)
                pool.tensor_tensor(rstd2[:, :], mv2[:, :, 1], half[:, 0:QT], ALU.pow).then_inc(rstd2_ready, 1)
                pool.wait_ge(y2_ready, b * 2 + 2)
                for t in range(QT):
                    pool.tensor_tensor(res[:, t, :], y2[:, t, :], gamma_bc[:, :], ALU.mult).then_inc(res_steps, 1)
                pool.wait_ge(res_steps, b * 4 + 2)
                for t in range(QT):
                    pool.tensor_tensor(y2[:, t, :], res[:, t, :], beta_bc[:, :], ALU.add).then_inc(res_steps, 1)
                pool.wait_ge(res_steps, b * 4 + 4)
                xr = x_all[:, bass.ds(b * QT, QT), :]
                pool.tensor_tensor(xr, y2[:, :, :], xr, ALU.add).then_inc(tile_done, 1)

            steps(pool, step)

            def tile(s, par):
                if second(s):
                    pool.wait_ge(y_ready, s - 1)
                    pool.dma_start(y_slots[bass.ds((s - 2) * S, S), :].rearrange("(t p) d -> p t d", p=P), y[:, par, :, :]).then_inc(y_stored[par], 16)

            tiles(pool, tile)
            for u in range(2):
                pool.wait_ge(y_stored[u], 16 * (NS // 2))
            with pool.Fori(0, NT // 4) as i:
                for u in range(4):
                    t = i * 4 + u
                    pool.wait_ge(fin_step, i * 8 + (2 * u + 2))
                    pool.tensor_copy(back_i[:, u, :], slot_i[:, bass.ds(t, 1), :].rearrange("p a d -> p (a d)")).then_inc(back_ready, 1)
                    pool.wait_ge(back_ready, i * 4 + (u + 1))
                    pool.nop(nofuse=True)
                    for c in range(2):
                        pool.indirect_dma_start(out=got[:, u, c, :], out_offset=None, in_=y_slots,
                                                in_offset=bass.IndirectOffsetOnAxis(ap=back_i[:, u, c:c + 1], axis=0)).then_inc(got_ready[u], 16)

        @block.scalar
        def _(act):
            act.dma_start(wqkv[:, :], w_qkv).then_inc(weights_loaded, 16)
            act.dma_start(wp[:, :], w_proj).then_inc(weights_loaded, 16)
            act.dma_start(wr[:, :], w_router).then_inc(weights_loaded, 16)
            act.dma_start(bproj_bc[:, :], b_proj.rearrange("(o d) -> o d", o=1).to_broadcast([P, D])).then_inc(weights_loaded, 16)
            act.dma_start(gamma_bc[:, :], gamma.rearrange("(o d) -> o d", o=1).to_broadcast([P, D])).then_inc(weights_loaded, 16)
            act.dma_start(beta_bc[:, :], beta.rearrange("(o d) -> o d", o=1).to_broadcast([P, D])).then_inc(weights_loaded, 16)
            act.wait_ge(wrT_filled, 1)
            act.activation(wrT[:, :], bank["head"][:, 0:E], ACT.Copy).then_inc(wrT_ready, 1)
            with act.Fori(0, LOOP2) as i:
                for k in range(2):
                    act.wait_ge(stage_T_filled, i * 2 + (k + 1))
                    act.activation(stage_T[:, k, :], bank[("maxA", "maxB")[k]][:, :], ACT.Copy).then_inc(stage_T_ready, 1)

            act.wait_ge(route, 2)
            act.activation(prob[:, :, :], prob2[:, :, :], ACT.Exp).then_inc(exp_router, 1)

            def exp(s, u):
                ps, free = wait_full(act, s, f"s{u}")
                act.activation(probs[:, u, :], ps[:, :], ACT.Exp, scale=SCALE).then_inc(exp_ready, 1)
                act.wait_ge(exp_ready, (s - 1) * 6 + (u + 1))
                act.nop().then_inc(free, 1)

            def step(s, par):
                front, back = FRONT in halves(s), BACK in halves(s)
                if front:
                    ps, free = wait_full(act, s, "xT")
                    act.activation(xbT[:, par, :], ps[:, 0:T], ACT.Copy).then_inc(xbT_ready, 1)
                    act.wait_ge(xbT_ready, s + 1)
                    act.nop().then_inc(free, 1)
                if back:
                    exp(s, 0)
                    exp(s, 1)
                if front:
                    ps, _ = wait_full(act, s, "q")
                    act.activation(q_hi[:, :], ps[:, :], ACT.Copy).then_inc(hi_ready, 1)
                    ps, _ = wait_full(act, s, "k")
                    act.activation(k_hi[:, :], ps[:, :], ACT.Identity, bias=k_one[:, :]).then_inc(hi_ready, 1)
                if back:
                    exp(s, 2)
                    exp(s, 3)
                    exp(s, 4)
                    for half_ in range(2):
                        if half_:
                            exp(s, 5)
                        ps, free = wait_full(act, s, f"o{half_}")
                        act.activation(o_T[:, 2 * half_:2 * half_ + 2, :], ps[:, :], ACT.Copy).then_inc(o_T_ready, 1)
                        act.wait_ge(o_T_ready, (s - 1) * 2 + (half_ + 1))
                        act.nop().then_inc(free, 1)
                if front:
                    ps, _ = wait_full(act, s, "shift")
                    act.activation(shift_T[:, 0, :], ps[0:H, 0:T], ACT.Copy, scale=1.0 / SHIFT_UNIT).then_inc(shift_hi_ready, 1)
                if back:
                    ps, free = wait_full(act, s, "onT")
                    act.activation(o_nT[:, :], ps[:, 0:T], ACT.Copy).then_inc(o_nT_ready, 1)
                    act.wait_ge(o_nT_ready, (s - 1) * 1 + 1)
                    act.nop().then_inc(free, 1)

            steps(act, step)

            act.wait_ge(route, ROUTE_DONE)
            act.wait_ge(expert_weights, 48)
            act.wait_ge(attention_done, 1)

            def tile(s, par):
                if not first(s):
                    return
                e = act.value_load(expert_i[0:1, bass.ds(s, 1)], min_val=0, max_val=E - 1)
                act.wait_ge(h_filled, s + 1)
                for c in range(HC):
                    act.activation(hT[:, par, c, :], wide[par][:, S * c:S * (c + 1)], ACT.Gelu,
                                   bias=b1_all[:, bass.ds(e, 1), c:c + 1].rearrange("p a b -> p (a b)")).then_inc(h_ready, 1)

            tiles(act, tile)

        @block.vector
        def _(dve):
            V = nc.vector
            n = NT // 4
            dve.wait_ge(weights_loaded, 96)
            dve.wait_ge(consts, 19)
            for dst, o in ((wq_rep, 0), (wk_rep, D)):
                src = wqkv[:, o:o + D].rearrange("p (g j d) -> p g j d", g=G, j=J)
                for g in range(G):
                    for t in range(3):
                        V.tensor_copy(dst[:, g, :].rearrange("p (j r) -> p j r", j=J)[:, :, HD * t:HD * (t + 1)],
                                      src[:, g, :, :]).then_inc(prep, 1)
            V.tensor_scalar(k_low[:, :], row_col[:, :], 32.0, -32.0, ALU.is_ge, ALU.mult).then_inc(prep, 1)
            V.tensor_scalar(k_one[:, :], row_col[:, :], 64.0, -32.0, ALU.is_ge, ALU.mult).then_inc(prep, 1)
            V.tensor_scalar(q_low[:, :], row_col[:, :], 96.0, -32.0, ALU.is_ge, ALU.mult).then_inc(prep, 1)
            dve.wait_ge(prep, 27)
            for i_, o in enumerate((k_low, k_one, q_low)):
                V.tensor_tensor(row_col[:, :], row_col[:, :], o[:, :], ALU.add).then_inc(prep, 1)
                dve.wait_ge(prep, 28 + i_)
            for c, edge in enumerate((8.0, 16.0, 24.0, 26.0)):
                V.tensor_scalar(row_id[:, c:c + 1], row_col[:, :], edge, None, ALU.is_ge).then_inc(prep, 1)
            dve.wait_ge(prep, 34)
            ge8, ge16, ge24, ge26 = (row_id[:, c:c + 1] for c in range(4))
            V.tensor_tensor(q_low[:, :], ge24, ge16, ALU.subtract).then_inc(prep, 1)
            V.tensor_tensor(k_low[:, :], ge16, ge8, ALU.subtract).then_inc(prep, 1)
            V.tensor_tensor(k_one[:, :], ge24, ge26, ALU.subtract).then_inc(prep, 1)
            dve.wait_ge(prep, 37)
            V.tensor_tensor(k_low[:, :], k_low[:, :], k_one[:, :], ALU.add).then_inc(prep, 1)
            dve.wait_ge(prep, 38)
            V.tensor_scalar(k_one[:, :], k_one[:, :], SHIFT_UNIT, None, ALU.mult).then_inc(prep, 1)

            for c in range(4):
                dve.wait_ge(x_loaded[c], 16)
                with dve.Fori(c * n, (c + 1) * n) as t:
                    V.bn_stats(stats[:, bass.ds(t, 1), :].rearrange("p a s -> p (a s)"),
                               x_all[:, bass.ds(t, 1), :].rearrange("p a d -> p (a d)")).then_inc(prep, 1)
            dve.wait_ge(prep, 39 + NT)
            k0 = 39 + NT
            me, mo, se, so = (stats[:, :, c] for c in (1, 4, 2, 5))
            V.tensor_tensor(mean[:, :], me, mo, ALU.add).then_inc(prep, 1)
            V.tensor_tensor(dev[:, :], me, mo, ALU.subtract).then_inc(prep, 1)
            V.tensor_tensor(var[:, :], se, so, ALU.add).then_inc(prep, 1)
            dve.wait_ge(prep, k0 + 3)
            V.tensor_tensor(dev[:, :], dev[:, :], dev[:, :], ALU.mult).then_inc(prep, 1)
            V.tensor_scalar(mean[:, :], mean[:, :], 0.5, None, ALU.mult).then_inc(prep, 1)
            dve.wait_ge(prep, k0 + 5)
            V.scalar_tensor_tensor(out=var[:, :], in0=dev[:, :], scalar=D / 4.0, in1=var[:, :],
                                   op0=ALU.mult, op1=ALU.add).then_inc(prep, 1)
            dve.wait_ge(prep, k0 + 6)
            V.tensor_scalar(var[:, :], var[:, :], 1.0 / D, LN_EPS, ALU.mult, ALU.add).then_inc(var_ready, 1)
            dve.wait_ge(rstd_ready, 1)
            with dve.Fori(0, LOOP2) as i:
                for k in range(2):
                    for u in range(4):
                        t = i * 8 + (4 * k + u)
                        ins = V.tensor_scalar(stage[:, k, u, :], x_all[:, bass.ds(t, 1), :].rearrange("p a d -> p (a d)"),
                                              mean[:, bass.ds(t, 1)], rstd[:, bass.ds(t, 1)], ALU.subtract, ALU.mult)
                    ins.then_inc(staged, 1)
                    dve.wait_ge(stage_T_filled, i * 2 + (k + 1))
                    dve.wait_ge(stage_copied, i * 2 + (k + 1))
            route_count = 0

            def then(ins):
                nonlocal route_count
                route_count += 1
                ins.then_inc(route, 1)
                dve.wait_ge(route, route_count)

            def over_experts(a):
                return a.rearrange("p (t o) -> p t o", o=1).to_broadcast([P, NT, E])

            def over_tiles(a, n_):
                return a.rearrange("p (o e) -> p o e", o=1).to_broadcast([P, n_, E])

            dve.wait_ge(logits_filled, NT)
            lg = bank["misc"][:, :].rearrange("p (t e) -> p t e", e=E)
            then(V.tensor_reduce(red[:, :], lg, axis=AX.X, op=ALU.max))
            then(V.tensor_tensor(prob2[:, :, :], lg, over_experts(red[:, :]), ALU.subtract))
            dve.wait_ge(exp_router, 1)
            then(V.tensor_reduce(red[:, :], prob[:, :, :], axis=AX.X, op=ALU.add))
            then(V.reciprocal(red[:, :], red[:, :]))
            then(V.tensor_tensor(prob[:, :, :], prob[:, :, :], over_experts(red[:, :]), ALU.mult))
            for c, pr in enumerate((prob, prob2)):
                then(V.tensor_reduce(top[:, c, :], pr[:, :, :], axis=AX.X, op=ALU.max))
                then(V.tensor_tensor(key[:, :, :], pr[:, :, :], over_experts(top[:, c, :]), ALU.is_equal))
                then(V.tensor_tensor(key[:, :, :], key[:, :, :], over_tiles(order[:, :], NT), ALU.mult))
                then(V.tensor_reduce(red[:, :], key[:, :, :], axis=AX.X, op=ALU.max))
                then(V.tensor_tensor(pick[:, c, :, :], over_tiles(order[:, :], NT), over_experts(red[:, :]), ALU.is_equal))
                if c == 0:
                    then(V.scalar_tensor_tensor(out=prob2[:, :, :].rearrange("p t e -> p (t e)"),
                                                in0=pick[:, 0, :, :].rearrange("p t e -> p (t e)"), scalar=-2.0,
                                                in1=prob[:, :, :].rearrange("p t e -> p (t e)"), op0=ALU.mult, op1=ALU.add))
            then(V.tensor_tensor(picked16[:, :, :], pick[:, 0, :, :], pick[:, 1, :, :], ALU.add))
            assert route_count == ROUTE_PICKED
            dve.wait_ge(route_counts, 1)
            then(V.tensor_copy(total[:, :, :], bank["maxB"][:, :].rearrange("p (t e) -> p t e", e=E)))
            for e in range(E):
                V.tensor_tensor_scan(rank[:, :, e], ones[:, :], total[:, :, e], 0.0, ALU.mult, ALU.add).then_inc(route, 1)
                route_count += 1
            dve.wait_ge(route, route_count)
            then(V.tensor_scalar(padded_i[:, :], rank[:, NT - 1, :], float(S - 1), None, ALU.add))
            bits = S.bit_length() - 1
            then(V.tensor_scalar(padded_i[:, :], padded_i[:, :], bits, None, ALU.logical_shift_right))
            then(V.tensor_scalar(padded[:, :], padded_i[:, :], float(S), None, ALU.mult))
            then(V.tensor_tensor_scan(ends[:, :], ones[:, 0:E], padded[:, :], 0.0, ALU.mult, ALU.add))
            then(V.tensor_tensor(padded[:, :], ends[:, :], padded[:, :], ALU.subtract))
            then(V.tensor_tensor(rank[:, :, :], rank[:, :, :], total[:, :, :], ALU.subtract))
            then(V.tensor_tensor(rank[:, :, :], bank["maxA"][:, :].rearrange("p (t e) -> p t e", e=E), rank[:, :, :], ALU.add))
            then(V.tensor_tensor(rank[:, :, :], rank[:, :, :], over_tiles(padded[:, :], NT), ALU.add))
            for c in range(2):
                then(V.tensor_tensor(key[:, :, :], pick[:, c, :, :], rank[:, :, :], ALU.mult))
                then(V.tensor_reduce(slot[:, c, :], key[:, :, :], axis=AX.X, op=ALU.add))
                then(V.tensor_copy(slot_i[:, :, c], slot[:, c, :]))
            then(V.tensor_tensor(past[:, :, :], tile_start[:, :].rearrange("p (t o) -> p t o", o=1).to_broadcast([P, NS, E]),
                                 over_tiles(ends[:, :], NS), ALU.is_ge))
            then(V.tensor_reduce(expert[:, :], past[:, :, :], axis=AX.X, op=ALU.add))
            then(V.tensor_scalar(expert_i[:, :], expert[:, :], float(E - 1), None, ALU.min))
            assert route_count == ROUTE_DONE, route_count

            def split(s, par, what, hi, low, dst, ready, count):
                ps, free = wait_full(dve, s, what)
                dve.wait_ge(hi_ready, s * 2 + count)
                V.scalar_tensor_tensor(out=dst, in0=hi, scalar=low, in1=ps[:, :], op0=ALU.mult, op1=ALU.add).then_inc(ready, 1)
                dve.wait_ge(ready, s + 1)
                V.nop().then_inc(free, 1)

            def step(s, par):
                front, back = FRONT in halves(s), BACK in halves(s)
                if front:
                    split(s, par, "q", q_hi[:, :], q_low[:, :], q_cat[:, :, :].rearrange("p g t -> p (g t)"), q_cat_ready, 1)
                    split(s, par, "k", k_hi[:, :], k_low[:, :], k_cat[:, par, :, :].rearrange("p g t -> p (g t)"), k_cat_ready, 2)
                    ps, free = wait_full(dve, s, "v")
                    V.tensor_copy(v_aug[:, par, :, :, 0:HD],
                                  ps[:, 0:QT * D].rearrange("p (t h d) -> p t h d", t=QT, h=H)).then_inc(v_ready, 1)
                    dve.wait_ge(v_ready, s + 1)
                    V.nop().then_inc(free, 1)
                    for g in range(G):
                        for u in range(3):
                            ps, free = wait_full(dve, s, f"m{3 * g + u}")
                            if u == 0:
                                dst, keys, nh = shift[:, 0, :, g], P, 4
                            else:
                                dst, keys, nh = shift[:, 1, 2 * (u - 1):2 * u, g], T, 2
                            V.tensor_reduce(dst, ps[:, :].rearrange("p (j k) -> p j k", j=nh), axis=AX.X, op=ALU.max,
                                            negate=True).then_inc(shift_ready, 1)
                            dve.wait_ge(shift_ready, s * 12 + (3 * g + u + 1))
                            V.nop().then_inc(free, 1)
                if back:
                    b = s - 1
                    for t in range(QT):
                        ps, free = wait_full(dve, s, f"oT{t}")
                        heads = ps[:, :].rearrange("p (h r) -> p h r", r=ROWS)
                        V.reciprocal(rden[:, :], heads[:, :, HD]).then_inc(rden_ready, 1)
                        dve.wait_ge(rden_ready, b * 2 + (t + 1))
                        V.tensor_tensor(o_n[:, t, :, :], heads[:, :, 0:HD],
                                        rden[:, :].rearrange("p (h o) -> p h o", o=1).to_broadcast([P, H, HD]), ALU.mult).then_inc(o_n_ready, 1)
                        dve.wait_ge(o_n_ready, b * 2 + (t + 1))
                        V.nop().then_inc(free, 1)
                if front:
                    ps, free = wait_full(dve, s, "shift")
                    dve.wait_ge(shift_hi_ready, s + 1)
                    V.scalar_tensor_tensor(out=shift_T[:, 1, :], in0=ps[0:H, 0:T], scalar=1.0 / SHIFT_UNIT, in1=shift_T[:, 0, :],
                                           op0=ALU.mult, op1=ALU.subtract).then_inc(shift_T_ready, 1)
                    dve.wait_ge(shift_T_ready, s + 1)
                    V.nop().then_inc(free, 1)
                if back:
                    b = s - 1
                    ps, free = wait_full(dve, s, "proj")
                    dve.wait_ge(xpb_ready, b * 2 + 2)
                    V.tensor_tensor(x2[:, :, :], ps[:, 0:QT * D].rearrange("p (t d) -> p t d", t=QT), xpb[:, :, :], ALU.add).then_inc(x2_ready, 1)
                    dve.wait_ge(x2_ready, b * 1 + 1)
                    V.nop().then_inc(free, 1)
                    for t in range(QT):
                        V.bn_stats(st2[:, t, :], x2[:, t, :]).then_inc(st2_ready, 1)
                    dve.wait_ge(st2_ready, b * 2 + 2)
                    dve.nop(nofuse=True)
                    for t in range(QT):
                        V.bn_aggr(mv2[:, t, :], st2[:, t, :]).then_inc(mv2_ready, 1)
                    dve.wait_ge(mv2_ready, b * 3 + 2)
                    V.tensor_scalar(mv2[:, :, 1], mv2[:, :, 1], LN_EPS, None, ALU.add).then_inc(mv2_ready, 1)
                    dve.wait_ge(rstd2_ready, b * 1 + 1)
                    if not (isinstance(b, int) and b == 0):
                        dve.wait_ge(tile_done, b * 1)
                    for t in range(QT):
                        V.tensor_scalar(y2[:, t, :], x2[:, t, :], mv2[:, t, 0:1], rstd2[:, t:t + 1], ALU.subtract, ALU.mult).then_inc(y2_ready, 1)

            steps(dve, step)
            dve.wait_ge(tile_done, B)
            V.nop().then_inc(attention_done, 1)
            dve.wait_ge(expert_weights, 48)

            def tile(s, par):
                if first(s):
                    dve.wait_ge(xg_T_filled, s + 1)
                    V.tensor_copy(xgT[:, par, :], bank["misc"][:, 0:S]).then_inc(xg_T_ready, 1)
                if second(s):
                    e = dve.value_load(expert_i[0:1, bass.ds(s - 2, 1)], min_val=0, max_val=E - 1)
                    dve.wait_ge(y_filled, s - 1)
                    later(dve, y_stored[par], (s - (2 + par)) * 8, not isinstance(s, int) or s > 3)
                    V.tensor_tensor(y[:, par, :, :], bank["head"][:, 0:S].rearrange("p (t d) -> p t d", d=D),
                                    b2_bc[:, bass.ds(e, 1), :].to_broadcast([P, 2, D]), ALU.add).then_inc(y_ready, 1)

            tiles(dve, tile)
            V.nop().then_inc(fin_step, 8)
            for u in range(4):
                V.nop().then_inc(stored[u], 16)
            with dve.Fori(0, NT // 4) as i:
                for u in range(4):
                    t = i * 4 + u
                    dve.wait_ge(got_ready[u], i * 32 + 32)
                    dve.wait_ge(stored[u], i * 16 + 16)
                    V.scalar_tensor_tensor(out=fin[:, u, :], in0=got[:, u, 0, :], scalar=top[:, 0, bass.ds(t, 1)],
                                           in1=x_all[:, bass.ds(t, 1), :].rearrange("p a d -> p (a d)"), op0=ALU.mult, op1=ALU.add).then_inc(fin_step, 1)
                    dve.wait_ge(fin_step, i * 8 + (2 * u + 9))
                    V.scalar_tensor_tensor(out=fin[:, u, :], in0=got[:, u, 1, :], scalar=top[:, 1, bass.ds(t, 1)],
                                           in1=fin[:, u, :], op0=ALU.mult, op1=ALU.add).then_inc(fin_step, 1)
                    dve.wait_ge(fin_step, i * 8 + (2 * u + 10))
                    V.nop().then_inc(fin_ready, 1)

        @block.tensor
        def _(pe):
            M = nc.tensor.matmul
            pe.wait_ge(weights_loaded, 96)
            pe.wait_ge(consts, 19)
            nc.tensor.transpose(bank["head"][:, 0:E], wr[:, :], ident[0:E, 0:E]).then_inc(wrT_filled, 1)
            pe.wait_ge(wrT_ready, 1)
            with pe.Fori(0, LOOP2) as i:
                for k in range(2):
                    pe.wait_ge(staged, i * 2 + (k + 1))
                    ps = bank[("maxA", "maxB")[k]]
                    for u in range(4):
                        last = nc.tensor.transpose(ps[:, P * u:P * (u + 1)], stage[:, k, u, :], ident[:, :])
                    last.then_inc(stage_T_filled, 1)
                    pe.wait_ge(stage_T_ready, i * 2 + (k + 1))
                    for u in range(4):
                        t = i * 8 + (4 * k + u)
                        M(bank["misc"][:, bass.ds(t * E, E)], stage_T[:, k, P * u:P * (u + 1)], wrT[:, :],
                          start=True, stop=True).then_inc(logits_filled, 1)
            pe.wait_ge(route, ROUTE_PICKED)
            flat = picked16[:, :, :].rearrange("p t e -> p (t e)")
            M(bank["maxA"][:, :], before16[:, :], flat, start=True, stop=True)
            M(bank["maxB"][:, :], ones16[:, :], flat, start=True, stop=True).then_inc(route_counts, 1)
            pe.wait_ge(route, ROUTE_DONE)

            def step(s, par):
                back_par = 1 - par
                b = s - 1

                def scores(u):
                    ps, full = wait_room(pe, s, f"s{u}")
                    kt, gs = SCORES[u]
                    keys = k_cat[:, back_par, :, P * kt:P * (kt + 1)]
                    if kt == 0:
                        for h2 in range(2):
                            last = M(ps[:, 512 * h2:512 * (h2 + 1)], keys[:, gs[0], :],
                                     q_diag[:, back_par, gs[0], 2 * h2:2 * h2 + 2, :], start=True, stop=True)
                    else:
                        for n_, g in enumerate(gs):
                            last = M(ps[:, 512 * n_:512 * (n_ + 1)], keys[:, g, :],
                                     q_diag[:, back_par, g, :, P:T], start=True, stop=True)
                    last.then_inc(full, 1)

                def maxima(g):
                    for u in range(3):
                        ps, full = wait_room(pe, s, f"m{3 * g + u}")
                        qt, js, keys = (0, range(J), P) if u == 0 else (1, (2 * u - 2, 2 * u - 1), T)
                        for n_, j in enumerate(js):
                            M(ps[:, keys * n_:keys * (n_ + 1)], q_diag[:, par, g, j, P * qt:P * (qt + 1)],
                              k_cat[:, par, g, 0:keys], start=(n_ == 0), stop=False, skip_group_check=True)
                        nh = len(js)
                        dst = ps[:, :].rearrange("p (j k) -> p j k", j=nh)[:, :, keys - P:keys]
                        M(dst, ident16[:, :], mask16[:, :].rearrange("p (o k) -> p o k", o=1).to_broadcast([P, nh, P]),
                          start=False, stop=True, skip_group_check=True).then_inc(full, 1)

                def values(half_):
                    ps, full = wait_room(pe, s, f"o{half_}")
                    first = 3 * half_
                    pe.wait_ge(probs_ready, b * 6 + (first + 3))
                    for n_ in range(2):
                        g = 2 * half_ + n_
                        for kt in range(QT):
                            for j in range(J):
                                if kt == 0:
                                    p_, dst = probs[:, first + n_, T * j:T * (j + 1)], ps[32 * j:32 * (j + 1), T * n_:T * (n_ + 1)]
                                else:
                                    at = 512 * n_ + P * j
                                    p_, dst = probs[:, first + 2, at:at + P], ps[32 * j:32 * (j + 1), T * n_ + P:T * (n_ + 1)]
                                last = M(dst, v_aug[:, back_par, kt, J * g + j, :], p_, start=(kt == 0), stop=(kt == 1),
                                         skip_group_check=True)
                    last.then_inc(full, 1)

                front, back = FRONT in halves(s), BACK in halves(s)
                if front:
                    ps, full = wait_room(pe, s, "xT")
                    pe.wait_ge(xb_ready, s + 1)
                    for t in range(QT):
                        last = nc.tensor.transpose(ps[:, P * t:P * (t + 1)], xb[:, par, t, :], ident[:, :])
                    last.then_inc(full, 1)
                if back:
                    pe.wait_ge(shift_loaded, b * (32 * J) + 32 * J)
                    scores(0)
                    scores(1)
                if front:
                    pe.wait_ge(xbT_ready, s + 1)
                    for what, w in (("q", wq_rep), ("k", wk_rep)):
                        ps, full = wait_room(pe, s, what)
                        for g in range(G):
                            last = M(ps[:, T * g:T * (g + 1)], w[:, g, :], xbT[:, par, :], start=True, stop=True)
                        last.then_inc(full, 1)
                    ps, full = wait_room(pe, s, "v")
                    for t in range(QT):
                        last = M(ps[:, D * t:D * (t + 1)], xbT[:, par, P * t:P * (t + 1)], wqkv[:, 2 * D:3 * D], start=True, stop=True)
                    last.then_inc(full, 1)
                if back:
                    scores(2)
                    scores(3)
                if front:
                    pe.wait_ge(k_cat_ready, s + 1)
                    pe.wait_ge(q_diag_loaded, (s + 1) * (16 * J))
                    maxima(0)
                if back:
                    pe.wait_ge(v_ready, b * 1 + 1)
                    values(0)
                    scores(4)
                if front:
                    maxima(1)
                if back:
                    scores(5)
                if front:
                    maxima(2)
                if back:
                    values(1)
                if front:
                    maxima(3)
                if back:
                    for t in range(QT):
                        ps, full = wait_room(pe, s, f"oT{t}")
                        pe.wait_ge(o_T_ready, b * 2 + 2)
                        for g in range(G):
                            last = nc.tensor.transpose(ps[:, P * g:P * (g + 1)], o_T[:, g, P * t:P * (t + 1)], ident[:, :])
                        last.then_inc(full, 1)
                if front:
                    ps, full = wait_room(pe, s, "shift")
                    pe.wait_ge(shift_ready, s * 12 + 12)
                    for t in range(QT):
                        last = nc.tensor.transpose(ps[0:H, P * t:P * (t + 1)],
                                                   shift[:, t, :, :].rearrange("p j g -> p (j g)"), ident[:, :])
                    last.then_inc(full, 1)
                if back:
                    ps, full = wait_room(pe, s, "onT")
                    pe.wait_ge(o_n_ready, b * 2 + 2)
                    for t in range(QT):
                        last = nc.tensor.transpose(ps[:, P * t:P * (t + 1)], o_n[:, t, :, :].rearrange("p h d -> p (h d)"), ident[:, :])
                    last.then_inc(full, 1)
                    ps, full = wait_room(pe, s, "proj")
                    pe.wait_ge(o_nT_ready, b * 1 + 1)
                    for t in range(QT):
                        last = M(ps[:, D * t:D * (t + 1)], o_nT[:, P * t:P * (t + 1)], wp[:, :], start=True, stop=True)
                    last.then_inc(full, 1)

            steps(pe, step)

            pe.wait_ge(attention_done, 1)

            def tile(s, par):
                if first(s):
                    pe.wait_ge(xg_loaded[par], (s - par) * 8 + 16)
                    later(pe, xg_T_ready, s, not isinstance(s, int) or s > 0)
                    for t in range(2):
                        last = nc.tensor.transpose(bank["misc"][:, P * t:P * (t + 1)], xg[:, par, t, :], ident[:, :])
                    last.then_inc(xg_T_filled, 1)
                if second(s):
                    e = pe.value_load(expert_i[0:1, bass.ds(s - 2, 1)], min_val=0, max_val=E - 1)
                    pe.wait_ge(h_ready, s * HC - HC)
                    later(pe, y_ready, s - 2, not isinstance(s, int) or s > 2)
                    for t in range(2):
                        for c in range(HC):
                            last = M(bank["head"][:, D * t:D * (t + 1)], hT[:, par, c, P * t:P * (t + 1)],
                                     w2_all[:, bass.ds(e, 1), c, :].rearrange("p a d -> p (a d)"), start=(c == 0), stop=(c == HC - 1))
                    last.then_inc(y_filled, 1)
                if first(s):
                    pe.wait_ge(w1_loaded[par], (s - par) * 8 + 16)
                    pe.wait_ge(xg_T_ready, s + 1)
                    for c in range(HC):
                        last = M(wide[par][:, S * c:S * (c + 1)], w1b[:, par, P * c:P * (c + 1)], xgT[:, par, :], start=True, stop=True)
                    last.then_inc(h_filled, 1)

            tiles(pe, tile)


_INS = {
    "L0_attn_target": "x", "L0_attn_w_qkv": "w_qkv", "L0_attn_w_proj": "w_proj", "L0_attn_b_proj": "b_proj",
    "L0_attn_ln_gamma": "gamma", "L0_attn_ln_beta": "beta", "L0_ffn_Wr": "w_router",
    "L0_ffn_W1": "w1", "L0_ffn_b1": "b1", "L0_ffn_W2": "w2", "L0_ffn_b2": "b2",
}


def kernel(**inputs):
    import numpy as np
    from concourse import bacc
    from concourse.bass_utils import run_bass_kernel_spmd

    nc = bacc.Bacc("TRN2", target_bir_lowering=False, num_devices=1)
    arrays, args = {}, {}
    for name, short in _INS.items():
        a = np.ascontiguousarray(inputs[name])
        arrays[f"in_{short}"] = a
        args[short] = nc.dram_tensor(f"in_{short}", a.shape, mybir.dt.from_np(a.dtype), kind="ExternalInput").ap()
    out = nc.dram_tensor("out_0", inputs["L0_attn_target"].shape, F32, kind="ExternalOutput").ap()
    attention_and_moe(nc, out=out, **args)
    r = run_bass_kernel_spmd(nc, [arrays], core_ids=[0])
    return r.results[0]["out_0"]
```

```python
from contextlib import ExitStack

import concourse.bass as bass
from concourse import mybir

F32 = mybir.dt.float32
F16 = mybir.dt.float16
BF16 = mybir.dt.bfloat16
I32 = mybir.dt.int32
U32 = mybir.dt.uint32
ALU = mybir.AluOpType
ACT = mybir.ActivationFunctionType
AX = mybir.AxisListType

P = 128


def attention_and_moe(nc, x, w_qkv, w_proj, b_proj, gamma, beta, w_router, w1, b1, w2, b2, out):
    B, T, D = x.shape
    E, _, HID = w1.shape
    H = 16
    HD = D // H
    QT = T // P
    NT = B * QT
    HC = HID // P
    G, J = 4, 4
    ROWS = P // J
    SHIFT_ROW = 3
    LN_EPS = 1e-5
    SCALE = 1.0 / HD ** 0.5
    SHIFT_UNIT = 64.0
    MASKED = 32768.0
    S = 2 * P
    NS = B * T * 2 // S + E
    SW = D + 2
    NOWHERE = 1 << 29
    CHUNKS = 4
    TC = NT // CHUNKS
    assert D == P and QT == 2 and HD == 8 and G * J == H and ROWS == 4 * HD

    ctx = ExitStack()
    with ctx:
        def sb(name, shape, dt=F32):
            return ctx.enter_context(nc.sbuf_tensor(name, shape, dt))

        def sem(name):
            return ctx.enter_context(nc.semaphore(name))

        q_rows = nc.dram_tensor("q_rows", [2, P, 4, T], F16).ap()
        k_rows = nc.dram_tensor("k_rows", [2, P, 4, T], F16).ap()
        x_slots = nc.dram_tensor("x_slots", [NS * S, SW], F32).ap()

        x_all = sb("x_all", [P, NT, D])
        xn_all = sb("xn_all", [P, NT, D])
        ident = sb("ident", [P, P])
        ident16 = sb("ident16", [P, P], F16)
        mask16 = sb("mask16", [P, P], F16)
        wqkv = sb("wqkv", [P, 3 * D])
        wp = sb("wp", [P, D])
        wr = sb("wr", [E, D])
        wrT = sb("wrT", [P, E])
        bproj_bc = sb("bproj_bc", [P, D])
        gamma_bc = sb("gamma_bc", [P, D])
        beta_bc = sb("beta_bc", [P, D])
        head_edge = sb("head_edge", [P, H])
        is_edge = sb("is_edge", [P, 1])
        edge_rows = sb("edge_rows", [P, T], F16)
        zero_rows = sb("zero_rows", [P, T], F16)
        stats = sb("stats", [P, NT, 6])
        mean = sb("mean", [P, NT])
        var = sb("var", [P, NT])
        dev = sb("dev", [P, NT])
        rstd = sb("rstd", [P, NT])
        half = sb("half", [P, NT])
        stage = sb("stage", [P, 2, 4, D])
        stage_T = sb("stage_T", [P, 2, 4 * P])
        logits = sb("logits", [P, NT, E])

        xb = sb("xb", [P, 2, QT, D])
        xbT = sb("xbT", [P, 2, T])
        qk_hi = sb("qk_hi", [P, 2, T], F16)
        qk_lo = sb("qk_lo", [P, 2, T], F16)
        k_cat = sb("k_cat", [P, 2, G, T], F16)
        q_diag = sb("q_diag", [P, 2, G, J, T], F16)
        v_aug = sb("v_aug", [P, 2, QT, H, 32])
        shift = sb("shift", [P, QT, J, G])
        shift_T = sb("shift_T", [H, T], F16)
        probs = sb("probs", [P, 6, 2 * 512])
        o_T = sb("o_T", [P, G, T])
        rden = sb("rden", [P, H])
        o_n = sb("o_n", [P, QT, H, HD])
        o_nT = sb("o_nT", [P, T])
        xpb = sb("xpb", [P, QT, D])
        x2 = sb("x2", [P, QT, D])
        st2 = sb("st2", [P, QT, 6])
        mv2 = sb("mv2", [P, QT, 2])
        rstd2 = sb("rstd2", [P, QT])
        y2 = sb("y2", [P, QT, D])
        scaled = sb("scaled", [P, QT, D])
        res = sb("res", [P, 2, QT, D])

        prob2, key, total, rank = (probs[:, u, 0:NT * E].rearrange("p (t e) -> p t e", e=E) for u in range(4))
        past = probs[:, 4, 0:NS * E].rearrange("p (t e) -> p t e", e=E)
        prob = sb("prob", [P, NT, E])
        pick = sb("pick", [P, 2, NT, E])
        picked16 = sb("picked16", [P, NT, E], BF16)
        top = sb("top", [P, 2, NT])
        red = sb("red", [P, NT])
        order = sb("order", [P, E])
        before16 = sb("before16", [P, P], BF16)
        ones16 = sb("ones16", [P, P], BF16)
        ones = sb("ones", [P, NT])
        padded = sb("padded", [P, E])
        padded_i = sb("padded_i", [P, E], I32)
        ends = sb("ends", [P, E])
        tile_start = sb("tile_start", [P, NS])
        expert = sb("expert", [P, NS])
        expert_i = sb("expert_i", [P, NS], I32)
        slot = sb("slot", [P, 2, NT])
        slot_i = sb("slot_i", [P, NT, 2], U32)
        number = sb("number", [P, NT], I32)
        record = sb("record", [P, NT, 2, 2])
        fill = sb("fill", [P, NS * S // P // 16, SW])
        send = sb("send", [P, 2, 2, SW])
        send_i = sb("send_i", [P, 2, 2], U32)
        w2_all = sb("w2_all", [P, E, HC, D])
        b1_all = sb("b1_all", [P, E, HC])
        b2_bc = sb("b2_bc", [P, E, D])
        xg = sb("xg", [P, 4, 2, SW])
        xgT = sb("xgT", [P, 2, S])
        w1b = sb("w1b", [P, 2, HID])
        hT = probs[:, 0:4, :].rearrange("p (b c) (x s) -> p b (c x) s", b=2, s=S)
        yb = sb("yb", [P, 2, D])
        y = sb("y", [P, 2, 2, D])

        wide = [ctx.enter_context(nc.psum_tensor(f"wide{i}", [P, 1024], F32)) for i in range(2)]
        bank = {n: ctx.enter_context(nc.psum_tensor(f"bank_{n}", [P, 512], F32)) for n in ("maxA", "maxB", "head", "misc")}

        x_loaded = [sem(f"x_loaded{c}") for c in range(CHUNKS)]
        weights_loaded = sem("weights_loaded")
        consts = sem("consts")
        prep = sem("prep")
        edge_ready = sem("edge_ready")
        const_rows_stored = sem("const_rows_stored")
        var_ready = sem("var_ready")
        rstd_ready = sem("rstd_ready")
        staged = sem("staged")
        stage_copied = sem("stage_copied")
        stage_T_filled = sem("stage_T_filled")
        stage_T_ready = sem("stage_T_ready")
        wrT_filled = sem("wrT_filled")
        wrT_ready = sem("wrT_ready")
        logits_filled = sem("logits_filled")
        filled = {n: sem(f"filled_{n}") for n in ("wide0", "wide1", "maxA", "maxB", "head", "misc")}
        emptied = {n: sem(f"emptied_{n}") for n in filled}
        xb_ready = sem("xb_ready")
        qk_hi_ready = sem("qk_hi_ready")
        rows_stored = sem("rows_stored")
        half_loaded = [sem(f"half_loaded{h}") for h in range(2)]
        shift_loaded = sem("shift_loaded")
        probs_ready = sem("probs_ready")
        rden_ready = sem("rden_ready")
        xpb_ready = sem("xpb_ready")
        st2_ready = sem("st2_ready")
        mv2_ready = sem("mv2_ready")
        rstd2_ready = sem("rstd2_ready")
        y2_ready = sem("y2_ready")
        scaled_ready = sem("scaled_ready")
        res_ready = sem("res_ready")
        res_stored = [sem(f"res_stored{u}") for u in range(2)]
        expert_weights = sem("expert_weights")
        fill_ready = sem("fill_ready")
        slots_filled = sem("slots_filled")
        exp_router = sem("exp_router")
        route = sem("route")
        route_counts = sem("route_counts")
        send_ready = sem("send_ready")
        sent = [sem(f"sent{u}") for u in range(2)]
        xg_loaded = [sem(f"xg_loaded{u}") for u in range(4)]
        w1_loaded = [sem(f"w1_loaded{u}") for u in range(2)]
        xg_T_filled = sem("xg_T_filled")
        xg_T_ready = sem("xg_T_ready")
        h_filled = sem("h_filled")
        h_ready = sem("h_ready")
        y_filled = sem("y_filled")
        yb_ready = sem("yb_ready")
        y_ready = sem("y_ready")
        added = sem("added")

        PROJECT, MAXIMA, SOFT, FINISH, LAST = range(5)
        STAGES = 5
        USES = [
            ("head", "o1", FINISH),
            ("maxA", "m0", MAXIMA), ("maxB", "m1", MAXIMA),
            ("misc", "xT", PROJECT),
            ("maxA", "m2", MAXIMA), ("maxB", "m3", MAXIMA),
            ("misc", "oT0", FINISH),
            ("maxA", "m4", MAXIMA),
            ("wide0", "s0", SOFT),
            ("maxB", "m5", MAXIMA),
            ("misc", "v", MAXIMA),
            ("wide1", "s1", SOFT),
            ("maxA", "m6", MAXIMA),
            ("misc", "oT1", FINISH),
            ("maxB", "m7", MAXIMA),
            ("misc", "qk", PROJECT),
            ("maxA", "m8", MAXIMA),
            ("wide0", "s2", SOFT),
            ("maxB", "m9", MAXIMA),
            ("head", "onT", FINISH),
            ("maxA", "m10", MAXIMA),
            ("wide1", "s3", SOFT),
            ("maxB", "m11", MAXIMA),
            ("head", "o0", SOFT),
            ("wide0", "s4", SOFT),
            ("misc", "shift", MAXIMA),
            ("head", "proj", FINISH),
            ("wide1", "s5", SOFT),
        ]
        STAGE_OF = {what: stage for _, what, stage in USES}
        SCORES = [(0, (0,)), (0, (1,)), (1, (0, 1)), (0, (2,)), (0, (3,)), (1, (2, 3))]

        def has(s, stage):
            return 0 <= s - stage < B if isinstance(s, int) else True

        def use(s, what):
            name = next(n for n, w, _ in USES if w == what)
            mine = [(w, h) for n, w, h in USES if n == name]
            at = [w for w, h in mine if has(s, h)].index(what)
            per_stage = [(h, sum(x == h for _, x in mine)) for h in range(STAGES)]
            if isinstance(s, int):
                return name, at + sum(n * min(max(s - h, 0), B) for h, n in per_stage)
            return name, s * len(mine) + (at - sum(n * h for h, n in per_stage))

        def buf(name):
            return wide[int(name[-1])] if name.startswith("wide") else bank[name]

        def room(eng, s, what):
            name, before = use(s, what)
            if not isinstance(before, int) or before > 0:
                eng.wait_ge(emptied[name], before)
            return buf(name), filled[name]

        def full(eng, s, what):
            name, before = use(s, what)
            eng.wait_ge(filled[name], before + 1)
            return buf(name), emptied[name]

        def made(eng, s, what):
            name, before = use(s, what)
            eng.wait_ge(emptied[name], before + 1)

        def later(eng, sem_, count, when):
            if when:
                eng.wait_ge(sem_, count)

        def beyond(s, n):
            return s > n if isinstance(s, int) else True

        def steps(eng, step):
            first_whole = STAGES - 1
            count = (B - 1 - first_whole) // 2 * 2
            for s in range(first_whole):
                step(s, s % 2)
            with eng.Fori(0, count // 2) as i:
                for k in range(2):
                    step(i * 2 + (first_whole + k), k)
            for s in range(first_whole + count, B + STAGES - 1):
                step(s, s % 2)

        def tiles(eng, step):
            for s in range(4):
                step(s, s)
            with eng.Fori(0, (NS - 4) // 4) as i:
                for k in range(4):
                    step(i * 4 + (4 + k), k)
            step(NS, 0)
            step(NS + 1, 1)

        def first(s):
            return s < NS if isinstance(s, int) else True

        def second(s):
            return s >= 2 if isinstance(s, int) else True

        GROUPS = NT // 4
        ROUTE_PICKED = 18
        ROUTE_DONE = 46

        def groups(eng, body):
            for g in range(2):
                body(g, g)
            with eng.Fori(1, GROUPS // 2) as i:
                for k in range(2):
                    body(i * 2 + k, k)

        block = ctx.enter_context(nc.Block())

        @block.sync
        def _(sp):
            xt = x.rearrange("b (t p) d -> p (b t) d", p=P)
            for c in range(CHUNKS):
                sp.dma_start(x_all[:, c * TC:(c + 1) * TC, :], xt[:, c * TC:(c + 1) * TC, :]).then_inc(x_loaded[c], 16)
            sp.wait_ge(edge_ready, 1)
            for par in range(2):
                sp.dma_start(q_rows[par, :, SHIFT_ROW, :], zero_rows[:, :]).then_inc(const_rows_stored, 16)
                sp.dma_start(k_rows[par, :, SHIFT_ROW, :], edge_rows[:, :]).then_inc(const_rows_stored, 16)
            sp.wait_ge(fill_ready, 1)
            xs = x_slots.rearrange("(c p r) d -> c p (r d)", c=16, p=P)
            for c in range(16):
                sp.dma_start(xs[c, :, :], fill[:, :, :].rearrange("p r d -> p (r d)")).then_inc(slots_filled, 16)
            sp.dma_start(w2_all[:, :, :, :], w2.rearrange("e (c p) d -> p e c d", p=P)).then_inc(expert_weights, 16)
            with nc.allow_non_contiguous_dma(reason="biases by hidden unit, once"):
                sp.dma_start(b1_all[:, :, :], b1.rearrange("e (c p) -> p e c", p=P)).then_inc(expert_weights, 16)
            sp.dma_start(b2_bc[:, :, :], b2.rearrange("(o e) d -> o e d", o=1).to_broadcast([P, E, D])).then_inc(expert_weights, 16)
            sp.wait_ge(const_rows_stored, 64)

            def load_half(b, par, h):
                gs = slice(2 * h, 2 * h + 2)
                qr = q_rows[par, :, :, :].rearrange("(g j d) t q -> j (d t) g q", g=G, j=J)
                kr = k_rows[par, :, :, :].rearrange("(g jd) t q -> (jd t) g q", g=G)
                for j in range(J):
                    rows = slice(ROWS * j, ROWS * (j + 1))
                    sp.dma_start(q_diag[rows, par, gs, j, :], qr[j, :, gs, :]).then_inc(half_loaded[h], 16)
                sp.dma_start(k_cat[:, par, gs, :], kr[:, gs, :]).then_inc(half_loaded[h], 16)

            def step(s, par):
                if has(s, MAXIMA):
                    b = s - MAXIMA
                    if has(s - 1, SOFT):
                        name, before = use(s - 1, "s5")
                        sp.wait_ge(filled[name], before + 1)
                    sp.wait_ge(rows_stored, b * 64 + 64)
                    sp.nop(nofuse=True)
                    load_half(b, 1 - par, 1)
                if has(s, PROJECT):
                    made(sp, s, "qk")
                    sp.nop(nofuse=True)
                    for src, dst, at in ((qk_hi[:, 0, :], q_rows, slice(0, 2)), (qk_lo[:, 0, :], q_rows, slice(2, 3)),
                                         (qk_hi[:, 1, :], k_rows, slice(0, 3, 2)), (qk_lo[:, 1, :], k_rows, slice(1, 2))):
                        n_ = len(range(*at.indices(4)))
                        src = src.rearrange("p (o q) -> p o q", o=1)
                        if n_ > 1:
                            src = src.to_broadcast([P, n_, T])
                        sp.dma_start(dst[par, :, at, :], src).then_inc(rows_stored, 16)
                    if has(s, SOFT):
                        name, before = use(s, "s2")
                        sp.wait_ge(filled[name], before + 1)
                    sp.wait_ge(rows_stored, s * 64 + 64)
                    sp.nop(nofuse=True)
                    load_half(s, par, 0)
                if has(s, MAXIMA):
                    b = s - MAXIMA
                    made(sp, s, "shift")
                    sp.nop(nofuse=True)
                    for j in range(J):
                        row = ROWS * j + SHIFT_ROW
                        sp.dma_start(q_diag[row:row + 1, 1 - par, :, j, :], shift_T[G * j:G * (j + 1), :]).then_inc(shift_loaded, 16)
                if has(s, LAST):
                    b = s - LAST
                    sp.wait_ge(res_ready, b * 1 + 1)
                    sp.nop(nofuse=True)
                    sp.dma_start(out.rearrange("b (t p) d -> b p t d", p=P)[bass.ds(b, 1)].rearrange("o p t d -> (o p) t d"),
                                 res[:, par, :, :]).then_inc(res_stored[par], 16)

            steps(sp, step)

            for u in range(2):
                sp.wait_ge(sent[u], 32 * (NT // 2))

            def tile(s, quad):
                if not first(s):
                    return
                par = quad % 2
                e = sp.value_load(expert_i[0:1, bass.ds(s, 1)], min_val=0, max_val=E - 1)
                later(sp, added, s * 32 - 96, beyond(s, 3))
                sp.nop(nofuse=True)
                sp.dma_start(xg[:, quad, :, :], x_slots[bass.ds(s * S, S), :].rearrange("(t p) d -> p t d", p=P)).then_inc(xg_loaded[quad], 16)
                later(sp, h_filled, s - 1, second(s))
                sp.nop(nofuse=True)
                sp.dma_start(w1b[:, par, :], w1[bass.ds(e, 1), :, :].rearrange("o p h -> (o p) h")).then_inc(w1_loaded[par], 16)

            tiles(sp, tile)

        @block.gpsimd
        def _(pool):
            pool.memset(head_edge[:, :], 0.0).then_inc(consts, 1)
            pool.memset(zero_rows[:, :], 0.0).then_inc(consts, 1)
            pool.memset(ident[:, :], 0.0).then_inc(consts, 1)
            pool.memset(ident16[:, :], 0.0).then_inc(consts, 1)
            pool.memset(mask16[:, :], 0.0).then_inc(consts, 1)
            pool.memset(half[:, :], -0.5).then_inc(consts, 1)
            pool.memset(ones[:, :], 1.0).then_inc(consts, 1)
            pool.memset(ones16[:, :], 1.0).then_inc(consts, 1)
            pool.memset(before16[:, :], 1.0).then_inc(consts, 1)
            pool.wait_ge(consts, 9)
            pool.affine_select(out=head_edge[:, :], in_=head_edge[:, :], compare_op=ALU.not_equal, fill=1.0, base=0,
                               pattern=[[-HD, H]], channel_multiplier=1).then_inc(consts, 1)
            pool.affine_select(out=ident[:, :], in_=ident[:, :], compare_op=ALU.not_equal, fill=1.0, base=0,
                               pattern=[[-1, P]], channel_multiplier=1).then_inc(consts, 1)
            pool.affine_select(out=ident16[:, :], in_=ident16[:, :], compare_op=ALU.not_equal, fill=MASKED, base=0,
                               pattern=[[-1, P]], channel_multiplier=1).then_inc(consts, 1)
            pool.affine_select(out=mask16[:, :], in_=mask16[:, :], compare_op=ALU.is_ge, fill=-MASKED, base=0,
                               pattern=[[-1, P]], channel_multiplier=1).then_inc(consts, 1)
            pool.affine_select(out=before16[:, :], in_=before16[:, :], compare_op=ALU.is_gt, fill=0.0, base=0,
                               pattern=[[1, P]], channel_multiplier=-1).then_inc(consts, 1)
            pool.iota(order[:, :], pattern=[[-1, E]], base=E, channel_multiplier=0,
                      allow_small_or_imprecise_dtypes=True).then_inc(consts, 1)
            pool.iota(tile_start[:, :], pattern=[[S, NS]], base=0, channel_multiplier=0,
                      allow_small_or_imprecise_dtypes=True).then_inc(consts, 1)
            pool.iota(number[:, :], pattern=[[P, NT]], base=0, channel_multiplier=1).then_inc(consts, 1)

            def group(g, k):
                pool.wait_ge(staged, g + 1)
                pool.nop(nofuse=True)
                pool.tensor_copy(xn_all[:, bass.ds(g * 4, 4), :], stage[:, k, :, :]).then_inc(stage_copied, 1)

            for c in range(CHUNKS):
                pool.wait_ge(var_ready, c + 1)
                cols = slice(c * TC, (c + 1) * TC)
                pool.tensor_tensor(rstd[:, cols], var[:, cols], half[:, cols], ALU.pow).then_inc(rstd_ready, 1)
                if c == 0:
                    pool.memset(v_aug[:, :, :, :, :], 0.0).then_inc(consts, 1)
                    pool.wait_ge(consts, 18)
                    pool.memset(v_aug[:, :, :, :, HD:HD + 1], 1.0).then_inc(consts, 1)
                elif c == 1:
                    pool.memset(fill[:, :, :], 0.0).then_inc(consts, 1)
                    pool.wait_ge(consts, 20)
                    pool.memset(fill[:, :, D + 1].bitcast(I32), NOWHERE).then_inc(fill_ready, 1)
                elif c == 2:
                    pool.memset(q_diag[:, :, :, :, :], 0.0).then_inc(consts, 1)
            groups(pool, group)

            def copy_in(s, par):
                if beyond(s, 1):
                    full(pool, s - 2, "xT")
                    pool.nop(nofuse=True)
                pool.tensor_copy(xb[:, par, :, :], xn_all[:, bass.ds(s * QT, QT), :]).then_inc(xb_ready, 1)

            pool.wait_ge(stage_copied, GROUPS)
            copy_in(0, 0)

            def send_tile(t, u):
                later(pool, sent[u], (t - u) * 16, beyond(t, 1))
                pool.nop(nofuse=True)
                pool.tensor_copy(send[:, u, :, 0:D], xn_all[:, bass.ds(t, 1), :].to_broadcast([P, 2, D])).then_inc(send_ready, 1)
                pool.tensor_copy(send[:, u, :, D:SW].bitcast(I32),
                                 record[:, bass.ds(t, 1), :, :].rearrange("p o c r -> p (o c) r").bitcast(I32)).then_inc(send_ready, 1)
                pool.tensor_copy(send_i[:, u, :], slot_i[:, bass.ds(t, 1), :].rearrange("p a d -> p (a d)")).then_inc(send_ready, 1)
                pool.wait_ge(send_ready, t * 3 + 3)
                pool.nop(nofuse=True)
                for c in range(2):
                    pool.indirect_dma_start(out=x_slots, out_offset=bass.IndirectOffsetOnAxis(ap=send_i[:, u, c:c + 1], axis=0),
                                            in_=send[:, u, c, :], in_offset=None).then_inc(sent[u], 16)

            def mask(s, u):
                made(pool, s, f"s{u}")
                pool.nop(nofuse=True)
                n, width = (J, T) if SCORES[u][0] == 0 else (2 * J, P)
                part = probs[:, u, :].rearrange("p (j q) -> p j q", q=width)[:, :, 0:P]
                pool.affine_select(out=part, in_=part, compare_op=ALU.is_ge, fill=0.0, base=0,
                                   pattern=[[0, n], [1, P]], channel_multiplier=-1).then_inc(probs_ready, 1)

            def step(s, par):
                if isinstance(s, int) and s == 0:
                    pool.wait_ge(slots_filled, 256)
                    pool.wait_ge(route, ROUTE_DONE)
                if not isinstance(s, int) or s + 1 < B:
                    copy_in(s + 1, 1 - par)
                if has(s, SOFT):
                    mask(s, 0)
                if has(s, FINISH):
                    b = s - FINISH
                    if has(s - 1, FINISH):
                        made(pool, s - 1, "proj")
                    pool.tensor_tensor(xpb[:, :, :], xn_all[:, bass.ds(b * QT, QT), :],
                                       bproj_bc[:, :].rearrange("p (o d) -> p o d", o=1).to_broadcast([P, QT, D]), ALU.add).then_inc(xpb_ready, 1)
                if has(s, PROJECT):
                    send_tile(s * 2, 0)
                if has(s, SOFT):
                    mask(s, 1)
                    mask(s, 2)
                if has(s, LAST):
                    b = s - LAST
                    pool.wait_ge(y2_ready, b * 2 + 2)
                    pool.tensor_tensor(scaled[:, :, :], y2[:, :, :], gamma_bc[:, :].rearrange("p (o d) -> p o d", o=1).to_broadcast([P, QT, D]), ALU.mult).then_inc(scaled_ready, 1)
                    later(pool, res_stored[par], (b - par) * 8, beyond(b, 1))
                    pool.tensor_tensor(res[:, par, :, :], x_all[:, bass.ds(b * QT, QT), :],
                                       beta_bc[:, :].rearrange("p (o d) -> p o d", o=1).to_broadcast([P, QT, D]), ALU.add).then_inc(scaled_ready, 1)
                    pool.wait_ge(scaled_ready, b * 2 + 2)
                    pool.tensor_tensor(res[:, par, :, :], res[:, par, :, :], scaled[:, :, :], ALU.add).then_inc(res_ready, 1)
                if has(s, SOFT):
                    mask(s, 3)
                if has(s, PROJECT):
                    send_tile(s * 2 + 1, 1)
                if has(s, SOFT):
                    mask(s, 4)
                    mask(s, 5)
                if has(s, FINISH):
                    b = s - FINISH
                    pool.wait_ge(mv2_ready, b * 3 + 3)
                    pool.tensor_tensor(rstd2[:, :], mv2[:, :, 1], half[:, 0:QT], ALU.pow).then_inc(rstd2_ready, 1)

            steps(pool, step)

            for u in range(2):
                pool.wait_ge(res_stored[u], 16 * (B // 2))

            def tile(s, quad):
                if second(s):
                    par = quad % 2
                    pool.wait_ge(y_ready, s * 2 - 2)
                    later(pool, added, s * 32 - 64, beyond(s, 2))
                    pool.nop(nofuse=True)
                    for t in range(2):
                        pool.indirect_dma_start(out=out.rearrange("b t d -> (b t) d"),
                                                out_offset=bass.IndirectOffsetOnAxis(ap=xg[:, (quad + 2) % 4, t, D + 1:SW].bitcast(U32), axis=0),
                                                in_=y[:, par, t, :], in_offset=None, bounds_check=B * T - 1, oob_is_err=False,
                                                compute_op=ALU.add).then_inc(added, 16)

            tiles(pool, tile)
            pool.wait_ge(added, 32 * NS)

        @block.scalar
        def _(act):
            act.dma_start(wqkv[:, :], w_qkv).then_inc(weights_loaded, 16)
            act.dma_start(wp[:, :], w_proj).then_inc(weights_loaded, 16)
            act.dma_start(wr[:, :], w_router).then_inc(weights_loaded, 16)
            act.dma_start(bproj_bc[:, :], b_proj.rearrange("(o d) -> o d", o=1).to_broadcast([P, D])).then_inc(weights_loaded, 16)
            act.dma_start(gamma_bc[:, :], gamma.rearrange("(o d) -> o d", o=1).to_broadcast([P, D])).then_inc(weights_loaded, 16)
            act.dma_start(beta_bc[:, :], beta.rearrange("(o d) -> o d", o=1).to_broadcast([P, D])).then_inc(weights_loaded, 16)
            act.wait_ge(wrT_filled, 1)
            act.activation(wrT[:, :], bank["head"][:, 0:E], ACT.Copy).then_inc(wrT_ready, 1)

            def group(g, k):
                act.wait_ge(stage_T_filled, g + 1)
                act.activation(stage_T[:, k, :], bank[("maxA", "maxB")[k]][:, :], ACT.Copy).then_inc(stage_T_ready, 1)

            groups(act, group)
            act.wait_ge(route, 2)
            act.activation(prob[:, :, :], prob2[:, :, :], ACT.Exp).then_inc(exp_router, 1)

            def copy(s, what, dst, cols, rows=P, scale=1.0):
                ps, empty = full(act, s, what)
                act.activation(dst, ps[0:rows, 0:cols], ACT.Copy, scale=scale).then_inc(empty, 1)

            def exp(s, u):
                ps, empty = full(act, s, f"s{u}")
                act.activation(probs[:, u, :], ps[:, :], ACT.Exp, scale=SCALE).then_inc(empty, 1)

            def step(s, par):
                if has(s, FINISH):
                    ps, empty = full(act, s, "o1")
                    act.activation(o_T[:, 2:4, :], ps[:, :], ACT.Copy).then_inc(empty, 1)
                if has(s, PROJECT):
                    copy(s, "xT", xbT[:, par, :], T)
                if has(s, SOFT):
                    exp(s, 0)
                if has(s, MAXIMA):
                    ps, empty = full(act, s, "v")
                    act.activation(v_aug[:, 1 - par, :, :, 0:HD],
                                   ps[:, 0:QT * D].rearrange("p (t h d) -> p t h d", t=QT, h=H), ACT.Copy).then_inc(empty, 1)
                if has(s, SOFT):
                    exp(s, 1)
                if has(s, PROJECT):
                    ps, _ = full(act, s, "qk")
                    act.activation(qk_hi[:, :, :], ps[:, :], ACT.Copy).then_inc(qk_hi_ready, 1)
                if has(s, SOFT):
                    exp(s, 2)
                if has(s, FINISH):
                    copy(s, "onT", o_nT[:, :], T)
                if has(s, SOFT):
                    exp(s, 3)
                    ps, empty = full(act, s, "o0")
                    act.activation(o_T[:, 0:2, :], ps[:, :], ACT.Copy).then_inc(empty, 1)
                    exp(s, 4)
                if has(s, MAXIMA):
                    copy(s, "shift", shift_T[:, :], T, rows=H, scale=1.0 / SHIFT_UNIT)
                if has(s, SOFT):
                    exp(s, 5)

            steps(act, step)

            act.wait_ge(expert_weights, 48)

            def tile(s, quad):
                if not first(s):
                    return
                par = quad % 2
                e = act.value_load(expert_i[0:1, bass.ds(s, 1)], min_val=0, max_val=E - 1)
                act.wait_ge(h_filled, s + 1)
                for c in range(HC):
                    act.activation(hT[:, par, c, :], wide[par][:, S * c:S * (c + 1)], ACT.Gelu,
                                   bias=b1_all[:, bass.ds(e, 1), c:c + 1].rearrange("p a b -> p (a b)")).then_inc(h_ready, 1)

            tiles(act, tile)

        @block.vector
        def _(dve):
            V = nc.vector
            dve.wait_ge(consts, 17)
            V.tensor_reduce(is_edge[:, :], head_edge[:, :], axis=AX.X, op=ALU.max).then_inc(prep, 1)
            dve.wait_ge(prep, 1)
            V.tensor_scalar(edge_rows[:, :], zero_rows[:, :], is_edge[:, :], SHIFT_UNIT, ALU.add, ALU.mult).then_inc(edge_ready, 1)

            UN = 4
            count = 1
            for c in range(CHUNKS):
                dve.wait_ge(x_loaded[c], 16)
                with dve.Fori(0, TC // UN) as i:
                    for u in range(UN):
                        t = i * UN + (c * TC + u)
                        V.bn_stats(stats[:, bass.ds(t, 1), :].rearrange("p a s -> p (a s)"),
                                   x_all[:, bass.ds(t, 1), :].rearrange("p a d -> p (a d)")).then_inc(prep, 1)
                count += TC
                dve.wait_ge(prep, count)
                cols = slice(c * TC, (c + 1) * TC)
                me, mo, se, so = (stats[:, cols, k] for k in (1, 4, 2, 5))
                V.tensor_tensor(mean[:, cols], me, mo, ALU.add).then_inc(prep, 1)
                V.tensor_tensor(dev[:, cols], me, mo, ALU.subtract).then_inc(prep, 1)
                V.tensor_tensor(var[:, cols], se, so, ALU.add).then_inc(prep, 1)
                dve.wait_ge(prep, count + 3)
                V.tensor_tensor(dev[:, cols], dev[:, cols], dev[:, cols], ALU.mult).then_inc(prep, 1)
                V.tensor_scalar(mean[:, cols], mean[:, cols], 0.5, None, ALU.mult).then_inc(prep, 1)
                dve.wait_ge(prep, count + 5)
                V.scalar_tensor_tensor(out=var[:, cols], in0=dev[:, cols], scalar=D / 4.0, in1=var[:, cols],
                                       op0=ALU.mult, op1=ALU.add).then_inc(prep, 1)
                count += 6
                dve.wait_ge(prep, count)
                V.tensor_scalar(var[:, cols], var[:, cols], 1.0 / D, LN_EPS, ALU.mult, ALU.add).then_inc(var_ready, 1)

            dve.wait_ge(rstd_ready, CHUNKS)

            def group(g, k):
                later(dve, stage_T_filled, g - 1, beyond(g, 1))
                later(dve, stage_copied, g - 1, beyond(g, 1))
                for u in range(4):
                    t = g * 4 + u
                    ins = V.tensor_scalar(stage[:, k, u, :], x_all[:, bass.ds(t, 1), :].rearrange("p a d -> p (a d)"),
                                          mean[:, bass.ds(t, 1)], rstd[:, bass.ds(t, 1)], ALU.subtract, ALU.mult)
                ins.then_inc(staged, 1)

            groups(dve, group)

            route_count = 0

            def then(ins):
                nonlocal route_count
                route_count += 1
                ins.then_inc(route, 1)
                dve.wait_ge(route, route_count)

            def over_experts(a):
                return a.rearrange("p (t o) -> p t o", o=1).to_broadcast([P, NT, E])

            def over_tiles(a, n_):
                return a.rearrange("p (o e) -> p o e", o=1).to_broadcast([P, n_, E])

            dve.wait_ge(logits_filled, NT)
            lg = bank["misc"][:, :].rearrange("p (t e) -> p t e", e=E)
            then(V.tensor_reduce(red[:, :], lg, axis=AX.X, op=ALU.max))
            then(V.tensor_tensor(prob2[:, :, :], lg, over_experts(red[:, :]), ALU.subtract))
            dve.wait_ge(exp_router, 1)
            then(V.tensor_reduce(red[:, :], prob[:, :, :], axis=AX.X, op=ALU.add))
            then(V.reciprocal(red[:, :], red[:, :]))
            then(V.tensor_tensor(prob[:, :, :], prob[:, :, :], over_experts(red[:, :]), ALU.mult))
            for c, pr in enumerate((prob, prob2)):
                then(V.tensor_reduce(top[:, c, :], pr[:, :, :], axis=AX.X, op=ALU.max))
                then(V.tensor_tensor(key[:, :, :], pr[:, :, :], over_experts(top[:, c, :]), ALU.is_equal))
                then(V.tensor_tensor(key[:, :, :], key[:, :, :], over_tiles(order[:, :], NT), ALU.mult))
                then(V.tensor_reduce(red[:, :], key[:, :, :], axis=AX.X, op=ALU.max))
                then(V.tensor_tensor(pick[:, c, :, :], over_tiles(order[:, :], NT), over_experts(red[:, :]), ALU.is_equal))
                if c == 0:
                    then(V.scalar_tensor_tensor(out=prob2[:, :, :].rearrange("p t e -> p (t e)"),
                                                in0=pick[:, 0, :, :].rearrange("p t e -> p (t e)"), scalar=-2.0,
                                                in1=prob[:, :, :].rearrange("p t e -> p (t e)"), op0=ALU.mult, op1=ALU.add))
            then(V.tensor_tensor(picked16[:, :, :], pick[:, 0, :, :], pick[:, 1, :, :], ALU.add))
            then(V.tensor_copy(record[:, :, :, 0].rearrange("p t c -> p c t"), top[:, :, :]))
            assert route_count == ROUTE_PICKED, route_count
            dve.wait_ge(route_counts, 1)
            then(V.tensor_copy(total[:, :, :], wide[1][:, 512:1024].rearrange("p (t e) -> p t e", e=E)))
            for e in range(E):
                V.tensor_tensor_scan(rank[:, :, e], ones[:, :], total[:, :, e], 0.0, ALU.mult, ALU.add).then_inc(route, 1)
                route_count += 1
            dve.wait_ge(route, route_count)
            then(V.tensor_scalar(padded_i[:, :], rank[:, NT - 1, :], float(S - 1), None, ALU.add))
            then(V.tensor_scalar(padded_i[:, :], padded_i[:, :], S.bit_length() - 1, None, ALU.logical_shift_right))
            then(V.tensor_scalar(padded[:, :], padded_i[:, :], float(S), None, ALU.mult))
            then(V.tensor_tensor_scan(ends[:, :], ones[:, 0:E], padded[:, :], 0.0, ALU.mult, ALU.add))
            then(V.tensor_tensor(padded[:, :], ends[:, :], padded[:, :], ALU.subtract))
            then(V.tensor_tensor(rank[:, :, :], rank[:, :, :], total[:, :, :], ALU.subtract))
            then(V.tensor_tensor(rank[:, :, :], wide[1][:, 0:512].rearrange("p (t e) -> p t e", e=E), rank[:, :, :], ALU.add))
            then(V.tensor_tensor(rank[:, :, :], rank[:, :, :], over_tiles(padded[:, :], NT), ALU.add))
            for c in range(2):
                then(V.tensor_copy(record[:, :, c, 1].bitcast(I32), number[:, :]))
                then(V.tensor_tensor(key[:, :, :], pick[:, c, :, :], rank[:, :, :], ALU.mult))
                then(V.tensor_reduce(slot[:, c, :], key[:, :, :], axis=AX.X, op=ALU.add))
                then(V.tensor_copy(slot_i[:, :, c], slot[:, c, :]))
            then(V.tensor_tensor(past[:, :, :], tile_start[:, :].rearrange("p (t o) -> p t o", o=1).to_broadcast([P, NS, E]),
                                 over_tiles(ends[:, :], NS), ALU.is_ge))
            then(V.tensor_reduce(expert[:, :], past[:, :, :], axis=AX.X, op=ALU.add))
            then(V.tensor_scalar(expert_i[:, :], expert[:, :], float(E - 1), None, ALU.min))
            assert route_count == ROUTE_DONE, route_count

            def maximum(s, m):
                ps, empty = full(dve, s, f"m{m}")
                g, u = divmod(m, 3)
                if u == 0:
                    dst, nh = shift[:, 0, :, g], 4
                else:
                    dst, nh = shift[:, 1, 2 * (u - 1):2 * u, g], 2
                V.tensor_reduce(dst, ps[:, :].rearrange("p (j k) -> p j k", j=nh), axis=AX.X, op=ALU.max,
                                negate=True).then_inc(empty, 1)

            def normalise(s, t):
                ps, empty = full(dve, s, f"oT{t}")
                heads = ps[:, :].rearrange("p (h r) -> p h r", r=ROWS)
                V.reciprocal(rden[:, :], heads[:, :, HD]).then_inc(rden_ready, 1)
                dve.wait_ge(rden_ready, (s - FINISH) * 2 + (t + 1))
                V.tensor_tensor(o_n[:, t, :, :], heads[:, :, 0:HD],
                                rden[:, :].rearrange("p (h o) -> p h o", o=1).to_broadcast([P, H, HD]), ALU.mult).then_inc(empty, 1)

            def step(s, par):
                if has(s, MAXIMA):
                    for m in (0, 1):
                        maximum(s, m)
                if has(s, LAST):
                    b = s - LAST
                    dve.wait_ge(rstd2_ready, b * 1 + 1)
                    later(dve, scaled_ready, b * 2, beyond(b, 0))
                    for t in range(QT):
                        V.tensor_scalar(y2[:, t, :], x2[:, t, :], mv2[:, t, 0:1], rstd2[:, t:t + 1], ALU.subtract, ALU.mult).then_inc(y2_ready, 1)
                if has(s, MAXIMA):
                    for m in (2, 3):
                        maximum(s, m)
                if has(s, FINISH):
                    normalise(s, 0)
                if has(s, MAXIMA):
                    for m in (4, 5, 6):
                        maximum(s, m)
                if has(s, FINISH):
                    normalise(s, 1)
                if has(s, MAXIMA):
                    maximum(s, 7)
                if has(s, PROJECT):
                    ps, empty = full(dve, s, "qk")
                    dve.wait_ge(qk_hi_ready, s + 1)
                    V.tensor_tensor(qk_lo[:, :, :].rearrange("p c q -> p (c q)"), ps[:, :],
                                    qk_hi[:, :, :].rearrange("p c q -> p (c q)"), ALU.subtract).then_inc(empty, 1)
                if has(s, MAXIMA):
                    for m in (8, 9, 10, 11):
                        maximum(s, m)
                if has(s, FINISH):
                    b = s - FINISH
                    ps, empty = full(dve, s, "proj")
                    dve.wait_ge(xpb_ready, b * 1 + 1)
                    V.tensor_tensor(x2[:, :, :], ps[:, 0:QT * D].rearrange("p (t d) -> p t d", t=QT), xpb[:, :, :], ALU.add).then_inc(empty, 1)
                    made(dve, s, "proj")
                    for t in range(QT):
                        V.bn_stats(st2[:, t, :], x2[:, t, :]).then_inc(st2_ready, 1)
                    dve.wait_ge(st2_ready, b * 2 + 2)
                    dve.nop(nofuse=True)
                    for t in range(QT):
                        V.bn_aggr(mv2[:, t, :], st2[:, t, :]).then_inc(mv2_ready, 1)
                    dve.wait_ge(mv2_ready, b * 3 + 2)
                    V.tensor_scalar(mv2[:, :, 1], mv2[:, :, 1], LN_EPS, None, ALU.add).then_inc(mv2_ready, 1)

            steps(dve, step)
            dve.wait_ge(expert_weights, 48)

            def tile(s, quad):
                par = quad % 2
                if first(s):
                    dve.wait_ge(xg_T_filled, s + 1)
                    V.tensor_copy(xgT[:, par, :], bank[("misc", "maxA")[par]][:, 0:S]).then_inc(xg_T_ready, 1)
                if second(s):
                    e = dve.value_load(expert_i[0:1, bass.ds(s - 2, 1)], min_val=0, max_val=E - 1)
                    dve.wait_ge(y_filled, s - 1)
                    later(dve, y_ready, s * 2 - 4, beyond(s, 2))
                    V.tensor_tensor(yb[:, :, :], bank[("head", "maxB")[par]][:, 0:S].rearrange("p (t d) -> p t d", d=D),
                                    b2_bc[:, bass.ds(e, 1), :].to_broadcast([P, 2, D]), ALU.add).then_inc(yb_ready, 1)
                    dve.wait_ge(yb_ready, s - 1)
                    later(dve, added, s * 32 - 96, beyond(s, 3))
                    for t in range(2):
                        V.tensor_scalar(y[:, par, t, :], yb[:, t, :], xg[:, (quad + 2) % 4, t, D:D + 1], None, ALU.mult).then_inc(y_ready, 1)

            tiles(dve, tile)

        @block.tensor
        def _(pe):
            M = nc.tensor.matmul
            pe.wait_ge(weights_loaded, 96)
            pe.wait_ge(consts, 17)
            nc.tensor.transpose(bank["head"][:, 0:E], wr[:, :], ident[0:E, 0:E]).then_inc(wrT_filled, 1)
            pe.wait_ge(wrT_ready, 1)

            def router(g, k):
                pe.wait_ge(stage_T_ready, g + 1)
                for u in range(4):
                    t = g * 4 + u
                    M(bank["misc"][:, bass.ds(t * E, E)], stage_T[:, k, P * u:P * (u + 1)], wrT[:, :],
                      start=True, stop=True).then_inc(logits_filled, 1)

            def group(g, k):
                pe.wait_ge(staged, g + 1)
                ps = bank[("maxA", "maxB")[k]]
                for u in range(4):
                    last = nc.tensor.transpose(ps[:, P * u:P * (u + 1)], stage[:, k, u, :], ident[:, :])
                last.then_inc(stage_T_filled, 1)
                if beyond(g, 0):
                    router(g - 1, 1 - k)

            groups(pe, group)
            router(GROUPS - 1, 1)
            pe.wait_ge(route, ROUTE_PICKED)
            flat = picked16[:, :, :].rearrange("p t e -> p (t e)")
            M(wide[1][:, 0:512], before16[:, :], flat, start=True, stop=True)
            M(wide[1][:, 512:1024], ones16[:, :], flat, start=True, stop=True).then_inc(route_counts, 1)
            pe.wait_ge(route, ROUTE_DONE)

            def step(s, par):
                b = s - SOFT

                def scores(u):
                    ps, fill_ = room(pe, s, f"s{u}")
                    kt, gs = SCORES[u]
                    keys = k_cat[:, par, :, P * kt:P * (kt + 1)]
                    if kt == 0:
                        for h2 in range(2):
                            last = M(ps[:, 512 * h2:512 * (h2 + 1)], keys[:, gs[0], :],
                                     q_diag[:, par, gs[0], 2 * h2:2 * h2 + 2, :], start=True, stop=True)
                    else:
                        for n_, g in enumerate(gs):
                            last = M(ps[:, 512 * n_:512 * (n_ + 1)], keys[:, g, :],
                                     q_diag[:, par, g, :, P:T], start=True, stop=True)
                    last.then_inc(fill_, 1)

                def maxima(m):
                    ps, fill_ = room(pe, s, f"m{m}")
                    g, u = divmod(m, 3)
                    qt, js, keys = (0, range(J), P) if u == 0 else (1, (2 * u - 2, 2 * u - 1), T)
                    for n_, j in enumerate(js):
                        M(ps[:, keys * n_:keys * (n_ + 1)], q_diag[:, 1 - par, g, j, P * qt:P * (qt + 1)],
                          k_cat[:, 1 - par, g, 0:keys], start=(n_ == 0), stop=False, skip_group_check=True)
                    nh = len(js)
                    dst = ps[:, :].rearrange("p (j k) -> p j k", j=nh)[:, :, keys - P:keys]
                    M(dst, ident16[:, :], mask16[:, :].rearrange("p (o k) -> p o k", o=1).to_broadcast([P, nh, P]),
                      start=False, stop=True, skip_group_check=True).then_inc(fill_, 1)

                def values(half_, of, count):
                    ps, fill_ = room(pe, s, f"o{half_}")
                    first_ = 3 * half_
                    pe.wait_ge(probs_ready, count)
                    for n_ in range(2):
                        g = 2 * half_ + n_
                        for kt in range(QT):
                            for j in range(J):
                                if kt == 0:
                                    p_, dst = probs[:, first_ + n_, T * j:T * (j + 1)], ps[32 * j:32 * (j + 1), T * n_:T * (n_ + 1)]
                                else:
                                    at = 512 * n_ + P * j
                                    p_, dst = probs[:, first_ + 2, at:at + P], ps[32 * j:32 * (j + 1), T * n_ + P:T * (n_ + 1)]
                                last = M(dst, v_aug[:, of, kt, J * g + j, :], p_, start=(kt == 0), stop=(kt == 1),
                                         skip_group_check=True)
                    last.then_inc(fill_, 1)

                def transpose_x():
                    ps, fill_ = room(pe, s, "xT")
                    pe.wait_ge(xb_ready, s + 1)
                    for t in range(QT):
                        last = nc.tensor.transpose(ps[:, P * t:P * (t + 1)], xb[:, par, t, :], ident[:, :])
                    last.then_inc(fill_, 1)

                def project_qk():
                    made(pe, s, "xT")
                    ps, fill_ = room(pe, s, "qk")
                    for c in range(2):
                        last = M(ps[:, T * c:T * (c + 1)], wqkv[:, D * c:D * (c + 1)], xbT[:, par, :], start=True, stop=True)
                    last.then_inc(fill_, 1)

                def project_v():
                    ps, fill_ = room(pe, s, "v")
                    for t in range(QT):
                        last = M(ps[:, D * t:D * (t + 1)], xbT[:, 1 - par, P * t:P * (t + 1)], wqkv[:, 2 * D:3 * D], start=True, stop=True)
                    last.then_inc(fill_, 1)

                def transpose_sums(t):
                    ps, fill_ = room(pe, s, f"oT{t}")
                    if t == 0:
                        made(pe, s, "o1")
                    for g in range(G):
                        last = nc.tensor.transpose(ps[:, P * g:P * (g + 1)], o_T[:, g, P * t:P * (t + 1)], ident[:, :])
                    last.then_inc(fill_, 1)

                def transpose_shifts():
                    made(pe, s, "m10")
                    made(pe, s, "m11")
                    ps, fill_ = room(pe, s, "shift")
                    for t in range(QT):
                        last = nc.tensor.transpose(ps[0:H, P * t:P * (t + 1)],
                                                   shift[:, t, :, :].rearrange("p j g -> p (j g)"), ident[:, :])
                    last.then_inc(fill_, 1)

                def transpose_normed():
                    made(pe, s, "oT1")
                    ps, fill_ = room(pe, s, "onT")
                    for t in range(QT):
                        last = nc.tensor.transpose(ps[:, P * t:P * (t + 1)], o_n[:, t, :, :].rearrange("p h d -> p (h d)"), ident[:, :])
                    last.then_inc(fill_, 1)

                def project_out():
                    made(pe, s, "onT")
                    ps, fill_ = room(pe, s, "proj")
                    for t in range(QT):
                        last = M(ps[:, D * t:D * (t + 1)], o_nT[:, P * t:P * (t + 1)], wp[:, :], start=True, stop=True)
                    last.then_inc(fill_, 1)

                for _, what, stage_ in USES:
                    if not has(s, stage_):
                        continue
                    if what == "o1":
                        values(1, 1 - par, (s - FINISH) * 6 + 6)
                    elif what == "o0":
                        made(pe, s - 1, "v")
                        values(0, par, b * 6 + 3)
                    elif what[0] == "m":
                        if what in ("m0", "m6"):
                            pe.wait_ge(half_loaded[what == "m6"], (s - MAXIMA) * 80 + 80)
                        maxima(int(what[1:]))
                    elif what[0] == "s" and what != "shift":
                        if what == "s0":
                            pe.wait_ge(shift_loaded, b * (16 * J) + 16 * J)
                        scores(int(what[1:]))
                    elif what[:2] == "oT":
                        transpose_sums(int(what[2:]))
                    else:
                        {"xT": transpose_x, "qk": project_qk, "v": project_v, "shift": transpose_shifts,
                         "onT": transpose_normed, "proj": project_out}[what]()

            steps(pe, step)
            for name in filled:
                pe.wait_ge(emptied[name], B * sum(n == name for n, _, _ in USES))
            pe.wait_ge(expert_weights, 48)

            def tile(s, quad):
                par = quad % 2
                if first(s):
                    pe.wait_ge(xg_loaded[quad], (s - quad) * 4 + 16)
                    later(pe, xg_T_ready, s - 1, beyond(s, 1))
                    for t in range(2):
                        last = nc.tensor.transpose(bank[("misc", "maxA")[par]][:, P * t:P * (t + 1)], xg[:, quad, t, 0:D], ident[:, :])
                    last.then_inc(xg_T_filled, 1)
                if second(s):
                    e = pe.value_load(expert_i[0:1, bass.ds(s - 2, 1)], min_val=0, max_val=E - 1)
                    pe.wait_ge(h_ready, s * HC - HC)
                    later(pe, yb_ready, s - 3, beyond(s, 3))
                    for t in range(2):
                        for c in range(HC):
                            last = M(bank[("head", "maxB")[par]][:, D * t:D * (t + 1)], hT[:, par, c, P * t:P * (t + 1)],
                                     w2_all[:, bass.ds(e, 1), c, :].rearrange("p a d -> p (a d)"), start=(c == 0), stop=(c == HC - 1))
                    last.then_inc(y_filled, 1)
                if first(s):
                    pe.wait_ge(w1_loaded[par], (s - par) * 8 + 16)
                    pe.wait_ge(xg_T_ready, s + 1)
                    for c in range(HC):
                        last = M(wide[par][:, S * c:S * (c + 1)], w1b[:, par, P * c:P * (c + 1)], xgT[:, par, :], start=True, stop=True)
                    last.then_inc(h_filled, 1)

            tiles(pe, tile)


_INS = {
    "L0_attn_target": "x", "L0_attn_w_qkv": "w_qkv", "L0_attn_w_proj": "w_proj", "L0_attn_b_proj": "b_proj",
    "L0_attn_ln_gamma": "gamma", "L0_attn_ln_beta": "beta", "L0_ffn_Wr": "w_router",
    "L0_ffn_W1": "w1", "L0_ffn_b1": "b1", "L0_ffn_W2": "w2", "L0_ffn_b2": "b2",
}


def kernel(**inputs):
    import numpy as np
    from concourse import bacc
    from concourse.bass_utils import run_bass_kernel_spmd

    nc = bacc.Bacc("TRN2", target_bir_lowering=False, num_devices=1)
    arrays, args = {}, {}
    for name, short in _INS.items():
        a = np.ascontiguousarray(inputs[name])
        arrays[f"in_{short}"] = a
        args[short] = nc.dram_tensor(f"in_{short}", a.shape, mybir.dt.from_np(a.dtype), kind="ExternalInput").ap()
    out = nc.dram_tensor("out_0", inputs["L0_attn_target"].shape, F32, kind="ExternalOutput").ap()
    attention_and_moe(nc, out=out, **args)
    r = run_bass_kernel_spmd(nc, [arrays], core_ids=[0])
    return r.results[0]["out_0"]
```

```python
from contextlib import ExitStack

import concourse.bass as bass
from concourse import mybir

F32 = mybir.dt.float32
F16 = mybir.dt.float16
BF16 = mybir.dt.bfloat16
I32 = mybir.dt.int32
U32 = mybir.dt.uint32
ALU = mybir.AluOpType
ACT = mybir.ActivationFunctionType
AX = mybir.AxisListType

P = 128


def attention_and_moe(nc, x, w_qkv, w_proj, b_proj, gamma, beta, w_router, w1, b1, w2, b2, out):
    B, T, D = x.shape
    E, _, HID = w1.shape
    H = 16
    HD = D // H
    QT = T // P
    NT = B * QT
    HC = HID // P
    G, J = 4, 4
    ROWS = P // J
    SHIFT_ROW = 3
    LN_EPS = 1e-5
    SCALE = 1.0 / HD ** 0.5
    SHIFT_UNIT = 64.0
    MASKED = 32768.0
    S = 2 * P
    NS = B * T * 2 // S + E
    SW = D + 2
    NOWHERE = 1 << 29
    CHUNKS = 4
    TC = NT // CHUNKS
    assert D == P and QT == 2 and HD == 8 and G * J == H and ROWS == 4 * HD

    ctx = ExitStack()
    with ctx:
        def sb(name, shape, dt=F32):
            return ctx.enter_context(nc.sbuf_tensor(name, shape, dt))

        def sem(name):
            return ctx.enter_context(nc.semaphore(name))

        qk_rows = nc.dram_tensor("qk_rows", [2, 2, P, 4, T], F16).ap()
        parts_dram = nc.dram_tensor("parts_dram", [2 * B * T + NS * S, D], F32).ap()
        x_slots = nc.dram_tensor("x_slots", [NS * S, SW], F32).ap()

        x_all = sb("x_all", [P, NT, D])
        xn_all = sb("xn_all", [P, NT, D])
        xnT_all = sb("xnT_all", [P, NT * P])
        ident = sb("ident", [P, P])
        ident16 = sb("ident16", [P, P], F16)
        mask16 = sb("mask16", [P, P], F16)
        wqkv = sb("wqkv", [P, 3 * D])
        wp = sb("wp", [P, D])
        wr = sb("wr", [E, D])
        wrT = sb("wrT", [P, 32])
        lgT = sb("lgT", [P, 4 * P])
        bproj_bc = sb("bproj_bc", [P, D])
        gamma_bc = sb("gamma_bc", [P, D])
        beta_bc = sb("beta_bc", [P, D])
        head_edge = sb("head_edge", [P, H])
        is_edge = sb("is_edge", [P, 1])
        stats = sb("stats", [P, NT, 6])
        mean = sb("mean", [P, NT])
        var = sb("var", [P, NT])
        dev = sb("dev", [P, NT])
        rstd = sb("rstd", [P, NT])
        half = sb("half", [P, NT])
        stage = sb("stage", [P, 2, 4, D])
        stage_T = sb("stage_T", [P, 2, 4 * P])
        logits = sb("logits", [P, NT, E])

        xbT = sb("xbT", [P, 2, T])
        split = sb("split", [P, 2 * 4, T], F16)
        k_cat = sb("k_cat", [P, 2, G, T], F16)
        q_diag = sb("q_diag", [P, 2, G, J, T], F16)
        v_aug = sb("v_aug", [P, 2, QT, H, 32])
        shift = sb("shift", [P, QT, J, G])
        shift_T = sb("shift_T", [H, T], F16)
        probs = sb("probs", [P, 6, 2 * 512])
        o_T = sb("o_T", [P, G, T])
        rden = sb("rden", [P, H])
        o_n = sb("o_n", [P, QT, H, HD])
        o_nT = sb("o_nT", [P, T])
        xpb = sb("xpb", [P, QT, D])
        x2 = sb("x2", [P, QT, D])
        st2 = sb("st2", [P, QT, 6])
        mv2 = sb("mv2", [P, QT, 2])
        rstd2 = sb("rstd2", [P, QT])
        y2 = sb("y2", [P, QT, D])

        PIECES = E
        piece = (stage[:, :, :, :].rearrange("p a b d -> p (a b d)"), stage_T[:, :, :].rearrange("p a q -> p (a q)"))

        prob2, key, total, rank = (probs[:, u, 0:NT * E].rearrange("p (t e) -> p t e", e=E) for u in range(4))
        past = probs[:, 4, 0:NS * E].rearrange("p (t e) -> p t e", e=E)
        pick = probs[:, 5, :].rearrange("p (c t e) -> p c t e", c=2, e=E)
        prob = sb("prob", [P, NT, E])
        picked16 = sb("picked16", [P, NT, E], BF16)
        top = sb("top", [P, 2, NT])
        red = sb("red", [P, NT])
        order = sb("order", [P, E])
        before16 = sb("before16", [P, P], BF16)
        ones16 = sb("ones16", [P, P], BF16)
        one_rows = sb("one_rows", [2, P], F16)
        ones = sb("ones", [P, NT])
        padded = sb("padded", [P, E])
        padded_i = sb("padded_i", [P, E], I32)
        ends = sb("ends", [P, E])
        tile_start = sb("tile_start", [P, NS])
        expert = sb("expert", [P, NS])
        BITS = (E - 1).bit_length()
        UNROLL = 8
        FIELDS = UNROLL + 2
        RUNS = NS // UNROLL + 1
        assert NS % UNROLL == 0 and FIELDS * BITS < 31
        padded_experts = sb("padded_experts", [P, UNROLL * RUNS + 2])
        packed = sb("packed", [P, 2, RUNS])
        packed_i = sb("packed_i", [P, 2, RUNS], I32)
        slot = sb("slot", [P, 2, NT])
        slot_i = sb("slot_i", [P, NT, 2], U32)
        record = sb("record", [P, NT, 2, 2])
        fill = sb("fill", [P, NS * S // P // 16, SW])
        send = sb("send", [P, 2, 2, SW])
        send_i = sb("send_i", [P, 2, 2], U32)
        w_parts = xnT_all[:, 0:2 * E * HID].bitcast(F16).rearrange("p (w x) -> p w x", w=4)
        w1_parts = w_parts[:, 0:2, :].rearrange("p w (e h) -> p w e h", e=E)
        w2_parts = w_parts[:, 2:4, :].rearrange("p w (e c d) -> p w e c d", e=E, c=HC)
        b1_all = sb("b1_all", [P, E, HC])
        b2_twice = sb("b2_twice", [2, E, D])
        b2_high, b2_parts = (split[0:2, 4 * u:4 * u + 4, :].rearrange("p r q -> p (r q)").rearrange("p (e d) -> p e d", e=E)
                             for u in range(2))
        minus_row = sb("minus_row", [2, 1])
        xg = fill[:, 0:8, :].rearrange("p (b t) d -> p b t d", b=4)
        xgT = lgT[:, :].bitcast(F16).rearrange("p (b w s) -> p b w s", b=2, w=2)
        hT = probs[:, 0:2, :].rearrange("p b (c s) -> p b c s", s=S)
        hT_parts = probs[:, 2:4, :].bitcast(F16).rearrange("p b (w c s) -> p b w c s", w=2, s=S)
        y = o_T[:, :, :].rearrange("p (b g) (h d) -> p b (g h) d", b=2, d=D)[:, :, 0:2, :]
        spare_row = sb("spare_row", [P, NS * 2], I32)
        dest = sb("dest", [P, 4, 2], I32)
        weight = sb("weight", [P, 4, 2])
        LAST_CHUNKS, PART_BUFS = 8, 4
        LC = NT // LAST_CHUNKS
        parts = xn_all[:, :, :].rearrange("p (b t c) d -> p b t (c d)", b=PART_BUFS, c=2)

        wide = [ctx.enter_context(nc.psum_tensor(f"wide{i}", [P, 1024], F32)) for i in range(2)]
        bank = {n: ctx.enter_context(nc.psum_tensor(f"bank_{n}", [P, 512], F32)) for n in ("maxA", "maxB", "head", "misc")}

        x_loaded = [sem(f"x_loaded{c}") for c in range(CHUNKS)]
        weights_loaded = sem("weights_loaded")
        consts = sem("consts")
        prep = sem("prep")
        var_ready = sem("var_ready")
        rstd_ready = sem("rstd_ready")
        staged = sem("staged")
        stage_copied = sem("stage_copied")
        xnT_filled = sem("xnT_filled")
        xnT_ready = sem("xnT_ready")
        lgT_filled = sem("lgT_filled")
        lgT_ready = sem("lgT_ready")
        wrT_filled = sem("wrT_filled")
        wrT_ready = sem("wrT_ready")
        logits_filled = sem("logits_filled")
        logits_ready = sem("logits_ready")
        filled = {n: sem(f"filled_{n}") for n in ("wide0", "wide1", "maxA", "maxB", "head", "misc")}
        emptied = {n: sem(f"emptied_{n}") for n in filled}
        xbT_ready = sem("xbT_ready")
        piece_loaded = [sem(f"piece_loaded{u}") for u in range(2)]
        piece_high = sem("piece_high")
        piece_low = sem("piece_low")
        qk_hi_ready = sem("qk_hi_ready")
        qk_high_ready = sem("qk_high_ready")
        rows_stored = sem("rows_stored")
        half_loaded = [sem(f"half_loaded{h}") for h in range(2)]
        shift_loaded = sem("shift_loaded")
        probs_ready = sem("probs_ready")
        rden_ready = sem("rden_ready")
        xpb_ready = sem("xpb_ready")
        st2_ready = sem("st2_ready")
        mv2_ready = sem("mv2_ready")
        rstd2_ready = sem("rstd2_ready")
        y2_ready = sem("y2_ready")
        offset_ready = sem("offset_ready")
        res_ready = sem("res_ready")
        expert_weights = sem("expert_weights")
        fill_ready = sem("fill_ready")
        slots_filled = sem("slots_filled")
        exp_router = sem("exp_router")
        route = sem("route")
        route_counts = sem("route_counts")
        send_rows_ready = sem("send_rows_ready")
        send_ready = sem("send_ready")
        sent = [sem(f"sent{u}") for u in range(2)]
        xg_loaded = [sem(f"xg_loaded{u}") for u in range(4)]
        xg_T_filled = sem("xg_T_filled")
        xg_T_high = sem("xg_T_high")
        xg_T_ready = sem("xg_T_ready")
        h_filled = sem("h_filled")
        h_ready = sem("h_ready")
        h_high = sem("h_high")
        h_high_2 = sem("h_high_2")
        h_parts_ready = sem("h_parts_ready")
        y_filled = sem("y_filled")
        b2_ready = sem("b2_ready")
        xg_used = sem("xg_used")
        y_ready = sem("y_ready")
        placed = [sem(f"placed{u}") for u in range(4)]
        parts_loaded = [sem(f"parts_loaded{u}") for u in range(PART_BUFS)]
        parts_added = sem("parts_added")
        out_ready = sem("out_ready")
        out_stored = sem("out_stored")

        PROJECT, MAXIMA, SOFT, FINISH, LAST = range(5)
        SEND = SOFT
        STAGES = 5
        USES = [
            ("maxA", "m0", MAXIMA), ("maxB", "m1", MAXIMA), ("misc", "qk", PROJECT),
            ("head", "o1", FINISH), ("maxA", "m2", MAXIMA), ("maxB", "m3", MAXIMA),
            ("misc", "v", MAXIMA), ("maxA", "m4", MAXIMA), ("wide0", "s0", SOFT),
            ("maxB", "m5", MAXIMA), ("wide1", "s1", SOFT), ("misc", "oT0", FINISH),
            ("maxA", "m6", MAXIMA), ("maxB", "m7", MAXIMA), ("wide0", "s2", SOFT),
            ("misc", "oT1", FINISH), ("maxA", "m8", MAXIMA), ("maxB", "m9", MAXIMA),
            ("head", "onT", FINISH), ("wide1", "s3", SOFT), ("maxA", "m10", MAXIMA),
            ("wide0", "s4", SOFT), ("maxB", "m11", MAXIMA), ("head", "o0", SOFT),
            ("misc", "shift", MAXIMA), ("wide1", "s5", SOFT), ("head", "proj", FINISH),
        ]
        LAST_AFTER, COPY_AFTER, SUM_AFTER, SEND_AFTER = "shift", "m8", "s0", ("m0", "s2")
        SCORES = [(0, (0,)), (0, (1,)), (1, (0, 1)), (0, (2,)), (0, (3,)), (1, (2, 3))]

        def has(s, stage):
            return 0 <= s - stage < B if isinstance(s, int) else True

        def use(s, what):
            name = next(n for n, w, _ in USES if w == what)
            mine = [(w, h) for n, w, h in USES if n == name]
            at = [w for w, h in mine if has(s, h)].index(what)
            per_stage = [(h, sum(x == h for _, x in mine)) for h in range(STAGES)]
            if isinstance(s, int):
                return name, at + sum(n * min(max(s - h, 0), B) for h, n in per_stage)
            return name, s * len(mine) + (at - sum(n * h for h, n in per_stage))

        def buf(name):
            return wide[int(name[-1])] if name.startswith("wide") else bank[name]

        def room(eng, s, what):
            name, before = use(s, what)
            if not isinstance(before, int) or before > 0:
                eng.wait_ge(emptied[name], before)
            return buf(name), filled[name]

        def full(eng, s, what):
            name, before = use(s, what)
            eng.wait_ge(filled[name], before + 1)
            return buf(name), emptied[name]

        def made(eng, s, what):
            name, before = use(s, what)
            eng.wait_ge(emptied[name], before + 1)

        def later(eng, sem_, count, when):
            if when:
                eng.wait_ge(sem_, count)

        def beyond(s, n):
            return s > n if isinstance(s, int) else True

        def steps(eng, step, after=((), ())):
            first_whole = STAGES - 1
            count = (B - 1 - first_whole) // 2 * 2
            for s in range(first_whole):
                step(s, s % 2)
                for other in after[s] if s < len(after) else ():
                    other()
            with eng.Fori(0, count // 2) as i:
                for k in range(2):
                    step(i * 2 + (first_whole + k), k)
            for s in range(first_whole + count, B + STAGES - 1):
                step(s, s % 2)

        def experts_of(eng, i):
            return eng.value_load(packed_i[0:1, 0, bass.ds(i, 1)], min_val=0, max_val=(1 << FIELDS * BITS) - 1)

        def expert_of(experts, k, back):
            return (experts >> BITS * (k + 2 - back)) & (E - 1)

        def tiles(eng, step, load=True):
            experts = experts_of(eng, 0) if load else None
            for s in range(UNROLL):
                step(s, s, experts)
            with eng.Fori(0, NS // UNROLL - 1) as i:
                experts = experts_of(eng, i + 1) if load else None
                for k in range(UNROLL):
                    step(i * UNROLL + (UNROLL + k), k, experts)
            experts = experts_of(eng, NS // UNROLL) if load else None
            step(NS, 0, experts)
            step(NS + 1, 1, experts)

        def first(s):
            return s < NS if isinstance(s, int) else True

        def hides(s):
            return 1 <= s <= NS if isinstance(s, int) else True

        def pieces(s):
            first_piece = 2 * (s - (B - 1)) if isinstance(s, int) else PIECES
            return range(first_piece, first_piece + 2) if 0 <= first_piece < PIECES else ()

        def part_of(i, low):
            w, at = 2 * (2 * i // PIECES) + low, 2 * HID * (i % (PIECES // 2))
            return w_parts[:, w, at:at + 2 * HID]

        def second(s):
            return s >= 2 if isinstance(s, int) else True

        GROUPS = NT // 4
        ROUTE_PICKED = 18
        ROUTE_DONE = 57

        def groups(eng, body):
            for q in range(4):
                body(q, q, 0)
            with eng.Fori(1, GROUPS // 4) as b:
                for q in range(4):
                    body(b * 4 + q, q, b)

        block = ctx.enter_context(nc.Block())

        @block.sync
        def _(sp):
            xt = x.rearrange("b (t p) d -> p (b t) d", p=P)
            for c in range(CHUNKS):
                sp.dma_start(x_all[:, c * TC:(c + 1) * TC, :], xt[:, c * TC:(c + 1) * TC, :]).then_inc(x_loaded[c], 16)
            sp.wait_ge(fill_ready, 1)
            xs = x_slots.rearrange("(c p r) d -> c p (r d)", c=16, p=P)
            for c in range(16):
                sp.dma_start(xs[c, :, :], fill[:, :, :].rearrange("p r d -> p (r d)")).then_inc(slots_filled, 16)
            with nc.allow_non_contiguous_dma(reason="biases by hidden unit, once"):
                sp.dma_start(b1_all[:, :, :], b1.rearrange("e (c p) -> p e c", p=P)).then_inc(expert_weights, 16)
            sp.dma_start(b2_twice[:, :, :], b2.rearrange("(o e) d -> o e d", o=1).to_broadcast([2, E, D])).then_inc(expert_weights, 16)
            def load_piece(i):
                w = w1[2 * i:2 * i + 2].rearrange("e p h -> p e h") if i < PIECES // 2 else \
                    w2[2 * i - PIECES:2 * i + 2 - PIECES].rearrange("e (c p) d -> p (e c) d", p=P)
                sp.dma_start(piece[i % 2].rearrange("p (a b) -> p a b", b=w.shape[2]), w).then_inc(piece_loaded[i % 2], 16)

            sp.wait_ge(logits_filled, GROUPS // 4)
            for i in range(2):
                load_piece(i)

            def load_half(b, par, h):
                gs = slice(2 * h, 2 * h + 2)
                qr = qk_rows[par, 0, :, :, :].rearrange("(g j d) t q -> j (d t) g q", g=G, j=J)
                kr = qk_rows[par, 1, :, :, :].rearrange("(g jd) t q -> (jd t) g q", g=G)
                for j in range(J):
                    rows = slice(ROWS * j, ROWS * (j + 1))
                    sp.dma_start(q_diag[rows, par, gs, j, :], qr[j, :, gs, :]).then_inc(half_loaded[h], 16)
                sp.dma_start(k_cat[:, par, gs, :], kr[:, gs, :]).then_inc(half_loaded[h], 16)

            def step(s, par):
                for i in pieces(s):
                    if i >= 2:
                        sp.wait_ge(piece_low, i - 1)
                        load_piece(i)
                if has(s, MAXIMA):
                    b = s - MAXIMA
                    if has(s - 1, SOFT):
                        name, before = use(s - 1, "s5")
                        sp.wait_ge(filled[name], before + 1)
                    sp.wait_ge(rows_stored, b * 16 + 16)
                    sp.nop(nofuse=True)
                    load_half(b, 1 - par, 1)
                if has(s, PROJECT):
                    made(sp, s, "qk")
                    sp.nop(nofuse=True)
                    sp.wait_ge(qk_high_ready, s + 1)
                    sp.nop(nofuse=True)
                    sp.dma_start(qk_rows[par, :, :, :, :].rearrange("c p t q -> p c (t q)"),
                                 split[:, :, :].rearrange("p (c t) q -> p c (t q)", c=2)).then_inc(rows_stored, 16)
                    if has(s, SOFT):
                        name, before = use(s, "s2")
                        sp.wait_ge(filled[name], before + 1)
                    sp.wait_ge(rows_stored, s * 16 + 16)
                    sp.nop(nofuse=True)
                    load_half(s, par, 0)
                if has(s, MAXIMA):
                    b = s - MAXIMA
                    made(sp, s, "shift")
                    sp.nop(nofuse=True)
                    for j in range(J):
                        row = ROWS * j + SHIFT_ROW
                        sp.dma_start(q_diag[row:row + 1, 1 - par, :, j, :], shift_T[G * j:G * (j + 1), :]).then_inc(shift_loaded, 16)

            steps(sp, step)

            for u in range(2):
                sp.wait_ge(sent[u], 32 * (NT // 2))

            def tile(s, k, experts):
                quad = k % 4
                if not first(s):
                    return
                later(sp, xg_used, s * 2 - 6, beyond(s, 3))
                sp.nop(nofuse=True)
                sp.dma_start(xg[:, quad, :, :], x_slots[bass.ds(s * S, S), :].rearrange("(t p) d -> p t d", p=P)).then_inc(xg_loaded[quad], 16)

            tiles(sp, tile, load=False)
            for u in range(4):
                sp.wait_ge(placed[u], 32 * (NS // 4))
            both = parts_dram[0:2 * B * T, :].rearrange("(t p c) d -> p t (c d)", p=P, c=2)
            for c in range(LAST_CHUNKS):
                if c >= PART_BUFS:
                    sp.wait_ge(out_ready, c - PART_BUFS + 1)
                sp.dma_start(parts[:, c % PART_BUFS, :, :], both[:, LC * c:LC * (c + 1), :]).then_inc(parts_loaded[c % PART_BUFS], 16)

        @block.gpsimd
        def _(pool):
            pool.memset(head_edge[:, :], 0.0).then_inc(consts, 1)
            pool.memset(wrT[:, :], 0.0).then_inc(consts, 1)
            pool.memset(padded_experts[:, :], 0.0).then_inc(consts, 1)
            pool.memset(split[:, :, :], 0.0).then_inc(consts, 1)
            pool.memset(ident[:, :], 0.0).then_inc(consts, 1)
            pool.memset(ident16[:, :], 0.0).then_inc(consts, 1)
            pool.memset(mask16[:, :], 0.0).then_inc(consts, 1)
            pool.memset(half[:, :], -0.5).then_inc(consts, 1)
            pool.memset(ones[:, :], 1.0).then_inc(consts, 1)
            pool.memset(ones16[:, :], 1.0).then_inc(consts, 1)
            pool.memset(one_rows[:, :], 1.0).then_inc(consts, 1)
            pool.memset(before16[:, :], 1.0).then_inc(consts, 1)
            pool.wait_ge(consts, 12)
            pool.affine_select(out=head_edge[:, :], in_=head_edge[:, :], compare_op=ALU.not_equal, fill=1.0, base=0,
                               pattern=[[-HD, H]], channel_multiplier=1).then_inc(consts, 1)
            pool.affine_select(out=ident[:, :], in_=ident[:, :], compare_op=ALU.not_equal, fill=1.0, base=0,
                               pattern=[[-1, P]], channel_multiplier=1).then_inc(consts, 1)
            pool.affine_select(out=ident16[:, :], in_=ident16[:, :], compare_op=ALU.not_equal, fill=MASKED, base=0,
                               pattern=[[-1, P]], channel_multiplier=1).then_inc(consts, 1)
            pool.affine_select(out=mask16[:, :], in_=mask16[:, :], compare_op=ALU.is_ge, fill=-MASKED, base=0,
                               pattern=[[-1, P]], channel_multiplier=1).then_inc(consts, 1)
            pool.affine_select(out=before16[:, :], in_=before16[:, :], compare_op=ALU.is_gt, fill=0.0, base=0,
                               pattern=[[1, P]], channel_multiplier=-1).then_inc(consts, 1)
            pool.iota(order[:, :], pattern=[[-1, E]], base=E, channel_multiplier=0,
                      allow_small_or_imprecise_dtypes=True).then_inc(consts, 1)
            pool.iota(tile_start[:, :], pattern=[[S, NS]], base=0, channel_multiplier=0,
                      allow_small_or_imprecise_dtypes=True).then_inc(consts, 1)
            for c in range(2):
                pool.iota(record[:, :, c, 1].bitcast(I32), pattern=[[2 * P, NT]], base=c, channel_multiplier=2).then_inc(consts, 1)
            pool.iota(minus_row[:, :], pattern=[[0, 1]], base=0, channel_multiplier=-1,
                      allow_small_or_imprecise_dtypes=True).then_inc(consts, 1)
            pool.iota(spare_row[:, :], pattern=[[P, NS * 2]], base=2 * B * T, channel_multiplier=1).then_inc(consts, 1)

            for c in range(CHUNKS):
                pool.wait_ge(var_ready, c + 1)
                cols = slice(c * TC, (c + 1) * TC)
                pool.tensor_tensor(rstd[:, cols], var[:, cols], half[:, cols], ALU.pow).then_inc(rstd_ready, 1)
                if c == 0:
                    pool.memset(fill[:, :, :], 0.0).then_inc(consts, 1)
                    pool.wait_ge(consts, 24)
                    pool.memset(fill[:, :, D + 1].bitcast(I32), NOWHERE).then_inc(fill_ready, 1)
                    pool.memset(q_diag[:, :, :, :, :], 0.0).then_inc(consts, 1)
                elif c == 1:
                    pool.memset(v_aug[:, :, :, :, :], 0.0).then_inc(consts, 1)
                    pool.wait_ge(consts, 26)
                    pool.memset(v_aug[:, :, :, :, HD:HD + 1], 1.0).then_inc(consts, 1)
            pool.wait_ge(stage_copied, GROUPS)

            def send_tile(t, u):
                later(pool, sent[u], (t - u) * 16, beyond(t, 1))
                pool.nop(nofuse=True)
                pool.tensor_copy(send[:, u, :, D:SW].bitcast(I32),
                                 record[:, bass.ds(t, 1), :, :].rearrange("p o c r -> p (o c) r").bitcast(I32)).then_inc(send_ready, 1)
                pool.tensor_copy(send_i[:, u, :], slot_i[:, bass.ds(t, 1), :].rearrange("p a d -> p (a d)")).then_inc(send_ready, 1)
                pool.wait_ge(send_rows_ready, t + 1)
                pool.wait_ge(send_ready, t * 2 + 2)
                pool.nop(nofuse=True)
                for c in range(2):
                    pool.indirect_dma_start(out=x_slots, out_offset=bass.IndirectOffsetOnAxis(ap=send_i[:, u, c:c + 1], axis=0),
                                            in_=send[:, u, c, :], in_offset=None).then_inc(sent[u], 16)

            def mask(s, u):
                made(pool, s, f"s{u}")
                pool.nop(nofuse=True)
                n, width = (J, T) if SCORES[u][0] == 0 else (2 * J, P)
                part = probs[:, u, :].rearrange("p (j q) -> p j q", q=width)[:, :, 0:P]
                pool.affine_select(out=part, in_=part, compare_op=ALU.is_ge, fill=0.0, base=0,
                                   pattern=[[0, n], [1, P]], channel_multiplier=-1).then_inc(probs_ready, 1)

            def sums(s):
                b = s - FINISH
                if has(s - 1, FINISH):
                    made(pool, s - 1, "proj")
                pool.tensor_tensor(xpb[:, :, :], xn_all[:, bass.ds(b * QT, QT), :],
                                   bproj_bc[:, :].rearrange("p (o d) -> p o d", o=1).to_broadcast([P, QT, D]), ALU.add).then_inc(xpb_ready, 1)
                pool.tensor_tensor(x_all[:, bass.ds(b * QT, QT), :], x_all[:, bass.ds(b * QT, QT), :],
                                   beta_bc[:, :].rearrange("p (o d) -> p o d", o=1).to_broadcast([P, QT, D]), ALU.add).then_inc(offset_ready, 1)

            def step(s, par):
                if isinstance(s, int) and s == SEND:
                    pool.wait_ge(slots_filled, 256)
                    pool.wait_ge(route, ROUTE_DONE)
                for _, what, stage_ in USES:
                    if what[0] == "s" and what != "shift" and has(s, SOFT):
                        mask(s, int(what[1:]))
                    if what in SEND_AFTER and has(s, SEND):
                        u = SEND_AFTER.index(what)
                        send_tile(s * 2 + (u - 2 * SEND), u)
                    if what == SUM_AFTER and has(s, FINISH):
                        sums(s)
                if has(s, FINISH):
                    b = s - FINISH
                    pool.wait_ge(mv2_ready, b * 3 + 3)
                    pool.tensor_tensor(rstd2[:, :], mv2[:, :, 1], half[:, 0:QT], ALU.pow).then_inc(rstd2_ready, 1)

            steps(pool, step)

            def tile(s, k, experts):
                quad = k % 4
                if second(s):
                    par = quad % 2
                    pool.wait_ge(y_ready, s * 2 - 2)
                    pool.nop(nofuse=True)
                    for t in range(2):
                        pool.indirect_dma_start(out=parts_dram, out_offset=bass.IndirectOffsetOnAxis(ap=dest[:, (quad + 2) % 4, t:t + 1].bitcast(U32), axis=0),
                                                in_=y[:, par, t, :], in_offset=None).then_inc(placed[(quad + 2) % 4], 16)

            tiles(pool, tile, load=False)

        @block.scalar
        def _(act):
            act.dma_start(wqkv[:, :], w_qkv).then_inc(weights_loaded, 16)
            act.dma_start(wp[:, :], w_proj).then_inc(weights_loaded, 16)
            act.dma_start(wr[:, :], w_router).then_inc(weights_loaded, 16)
            act.dma_start(bproj_bc[:, :], b_proj.rearrange("(o d) -> o d", o=1).to_broadcast([P, D])).then_inc(weights_loaded, 16)
            act.dma_start(gamma_bc[:, :], gamma.rearrange("(o d) -> o d", o=1).to_broadcast([P, D])).then_inc(weights_loaded, 16)
            act.dma_start(beta_bc[:, :], beta.rearrange("(o d) -> o d", o=1).to_broadcast([P, D])).then_inc(weights_loaded, 16)
            act.wait_ge(wrT_filled, 1)
            act.activation(wrT[:, 0:E], bank["head"][:, 0:E], ACT.Copy).then_inc(wrT_ready, 1)

            def rows_of_logits(b):
                act.wait_ge(lgT_filled, b + 1)
                act.activation(lgT[:, :], bank["misc"][:, :], ACT.Copy).then_inc(lgT_ready, 1)

            def logits_by_token(b):
                act.wait_ge(logits_filled, b + 1)
                act.activation(logits[:, bass.ds(b * 16, 16), :], bank["head"][:, :].rearrange("p (t r) -> p t r", r=32)[:, :, 0:E],
                               ACT.Copy).then_inc(logits_ready, 1)

            def group(g, q, b):
                act.wait_ge(staged, g + 1)
                act.activation(xn_all[:, bass.ds(g * 4, 4), :], stage[:, q % 2, :, :], ACT.Copy).then_inc(stage_copied, 1)
                act.wait_ge(xnT_filled, g + 1)
                act.activation(stage_T[:, q % 2, :], bank[("maxA", "maxB")[q % 2]][:, :], ACT.Copy).then_inc(xnT_ready, 1)
                act.activation(xnT_all[:, bass.ds(g * (4 * P), 4 * P)], bank[("maxA", "maxB")[q % 2]][:, :], ACT.Copy).then_inc(xnT_ready, 1)
                if q == 0 and beyond(b, 0):
                    rows_of_logits(b - 1)
                if q == 1 and beyond(b, 0):
                    logits_by_token(b - 1)

            groups(act, group)
            rows_of_logits(GROUPS // 4 - 1)
            logits_by_token(GROUPS // 4 - 1)
            def exp_of_logits():
                act.wait_ge(route, 2)
                act.activation(prob[:, :, :], prob2[:, :, :], ACT.Exp).then_inc(exp_router, 1)

            def copy(s, what, dst, cols, rows=P, scale=1.0):
                ps, empty = full(act, s, what)
                act.activation(dst, ps[0:rows, 0:cols], ACT.Copy, scale=scale).then_inc(empty, 1)

            def exp(s, u):
                ps, empty = full(act, s, f"s{u}")
                act.activation(probs[:, u, :], ps[:, :], ACT.Exp, scale=SCALE).then_inc(empty, 1)

            def copy_in(s, par):
                if has(s - 1, MAXIMA):
                    full(act, s - 1, "v")
                act.activation(xbT[:, par, :], xnT_all[:, bass.ds(s * T, T)], ACT.Copy).then_inc(xbT_ready, 1)

            def copy_send(t, u):
                later(act, sent[u], (t - u) * 16, beyond(t, 1))
                act.activation(send[:, u, :, 0:D], xn_all[:, bass.ds(t, 1), :].to_broadcast([P, 2, D]), ACT.Copy).then_inc(send_rows_ready, 1)

            act.wait_ge(xnT_ready, 2 * GROUPS)
            act.wait_ge(stage_copied, GROUPS)

            def step(s, par):
                for _, what, stage_ in USES:
                    if not has(s, stage_):
                        pass
                    elif what == "qk":
                        ps, _ = full(act, s, what)
                        later(act, rows_stored, s * 16, beyond(s, 0))
                        act.activation(split[:, 0:5:4, :], ps[:, :].rearrange("p (c q) -> p c q", c=2), ACT.Copy).then_inc(qk_hi_ready, 1)
                    elif what == "v":
                        ps, empty = full(act, s, what)
                        act.activation(v_aug[:, 1 - par, :, :, 0:HD],
                                       ps[:, 0:QT * D].rearrange("p (t h d) -> p t h d", t=QT, h=H), ACT.Copy).then_inc(empty, 1)
                    elif what in ("o0", "o1"):
                        ps, empty = full(act, s, what)
                        half_ = int(what[1:])
                        act.activation(o_T[:, 2 * half_:2 * half_ + 2, :], ps[:, :], ACT.Copy).then_inc(empty, 1)
                    elif what == "onT":
                        copy(s, what, o_nT[:, :], T)
                    elif what == "shift":
                        copy(s, what, shift_T[:, :], T, rows=H, scale=1.0 / SHIFT_UNIT)
                    elif what[0] == "s":
                        exp(s, int(what[1:]))
                    if what == COPY_AFTER and has(s, PROJECT):
                        copy_in(s, par)
                    if what in SEND_AFTER and has(s, SEND):
                        u = SEND_AFTER.index(what)
                        copy_send(s * 2 + (u - 2 * SEND), u)
                for i in pieces(s):
                    act.wait_ge(piece_loaded[i % 2], 16 * (i // 2 + 1))
                    act.activation(part_of(i, 0), piece[i % 2], ACT.Copy).then_inc(piece_high, 1)

            steps(act, step, after=((exp_of_logits,),))

            act.wait_ge(expert_weights, 32)

            def hidden(s, par, e, half_):
                act.wait_ge(h_filled, s * 2 + (half_ + 1))
                for c in range(HC // 2 * half_, HC // 2 * (half_ + 1)):
                    act.activation(hT[:, par, c, :], wide[par][:, S * c:S * (c + 1)], ACT.Gelu,
                                   bias=b1_all[:, bass.ds(e, 1), c:c + 1].rearrange("p a b -> p (a b)")).then_inc(h_ready, 1)

            def high_hidden(s, par, half_):
                cs = slice(HC // 2 * half_, HC // 2 * (half_ + 1))
                act.wait_ge(h_ready, s * HC + HC // 2 * (half_ + 1))
                act.activation(hT_parts[:, par, 0, cs, :], hT[:, par, cs, :], ACT.Copy).then_inc(h_high, 1)

            def tile(s, k, experts):
                quad = k % 4
                par = quad % 2
                if hides(s):
                    hidden(s - 1, 1 - par, expert_of(experts, k, 1), 0)
                if first(s):
                    act.wait_ge(xg_T_filled, s + 1)
                    act.activation(xgT[:, par, 0, :], bank[("misc", "maxA")[par]][:, 0:S], ACT.Copy).then_inc(xg_T_high, 1)
                if hides(s):
                    high_hidden(s - 1, 1 - par, 0)
                    hidden(s - 1, 1 - par, expert_of(experts, k, 1), 1)
                if second(s):
                    later(act, placed[quad], (s - quad) * 8, beyond(s, 3))
                    act.wait_ge(xg_used, s * 2 - 2)
                    act.wait_ge(y_filled, s - 1)
                    for t in range(2):
                        act.activation(y[:, par, t, :], bank[("head", "maxB")[par]][:, D * t:D * (t + 1)], ACT.Copy,
                                       scale=weight[:, (quad + 2) % 4, t:t + 1]).then_inc(y_ready, 1)

            tiles(act, tile)
            for c in range(LAST_CHUNKS):
                act.wait_ge(out_ready, c + 1)
                act.dma_start(out.rearrange("b (t p) d -> p (b t) d", p=P)[:, LC * c:LC * (c + 1), :],
                              x_all[:, LC * c:LC * (c + 1), :]).then_inc(out_stored, 16)
            act.wait_ge(out_stored, 16 * LAST_CHUNKS)

        @block.vector
        def _(dve):
            V = nc.vector
            dve.wait_ge(consts, 23)
            V.tensor_reduce(is_edge[:, :], head_edge[:, :], axis=AX.X, op=ALU.max).then_inc(prep, 1)
            dve.wait_ge(prep, 1)
            V.tensor_scalar(split[:, 7, :], split[:, 7, :], is_edge[:, :], SHIFT_UNIT, ALU.add, ALU.mult).then_inc(prep, 1)

            def normalise_group(g, k):
                later(dve, xnT_filled, g - 1, beyond(g, 1))
                later(dve, stage_copied, g - 1, beyond(g, 1))
                for u in range(4):
                    t = g * 4 + u
                    ins = V.tensor_scalar(stage[:, k, u, :], x_all[:, bass.ds(t, 1), :].rearrange("p a d -> p (a d)"),
                                          mean[:, bass.ds(t, 1)], rstd[:, bass.ds(t, 1)], ALU.subtract, ALU.mult)
                ins.then_inc(staged, 1)

            UN = 8
            count = 2
            CG = GROUPS // CHUNKS
            for c in range(CHUNKS + 1):
                if c == CHUNKS:
                    dve.wait_ge(rstd_ready, c)
                    with dve.Fori(0, CG // 2) as i:
                        for k in range(2):
                            normalise_group(i * 2 + (CG * (c - 1) + k), k)
                    break
                dve.wait_ge(x_loaded[c], 16)
                with dve.Fori(0, TC // UN) as i:
                    for u in range(UN):
                        t = i * UN + (c * TC + u)
                        V.bn_stats(stats[:, bass.ds(t, 1), :].rearrange("p a s -> p (a s)"),
                                   x_all[:, bass.ds(t, 1), :].rearrange("p a d -> p (a d)")).then_inc(prep, 1)
                count += TC
                dve.wait_ge(prep, count)
                cols = slice(c * TC, (c + 1) * TC)
                me, mo, se, so = (stats[:, cols, k] for k in (1, 4, 2, 5))
                V.tensor_tensor(mean[:, cols], me, mo, ALU.add).then_inc(prep, 1)
                V.tensor_tensor(dev[:, cols], me, mo, ALU.subtract).then_inc(prep, 1)
                V.tensor_tensor(var[:, cols], se, so, ALU.add).then_inc(prep, 1)
                dve.wait_ge(prep, count + 3)
                V.tensor_tensor(dev[:, cols], dev[:, cols], dev[:, cols], ALU.mult).then_inc(prep, 1)
                V.tensor_scalar(mean[:, cols], mean[:, cols], 0.5, None, ALU.mult).then_inc(prep, 1)
                dve.wait_ge(prep, count + 5)
                V.scalar_tensor_tensor(out=var[:, cols], in0=dev[:, cols], scalar=D / 4.0, in1=var[:, cols],
                                       op0=ALU.mult, op1=ALU.add).then_inc(prep, 1)
                count += 6
                dve.wait_ge(prep, count)
                V.tensor_scalar(var[:, cols], var[:, cols], 1.0 / D, LN_EPS, ALU.mult, ALU.add).then_inc(var_ready, 1)
                if c == 1:
                    dve.wait_ge(rstd_ready, c)
                    for g in range(CG):
                        normalise_group(g, g % 2)
                elif c > 1:
                    dve.wait_ge(rstd_ready, c)
                    with dve.Fori(0, CG // 2) as i:
                        for k in range(2):
                            normalise_group(i * 2 + (CG * (c - 1) + k), k)

            route_count = 0

            def then(ins):
                nonlocal route_count
                route_count += 1
                ins.then_inc(route, 1)
                dve.wait_ge(route, route_count)

            def over_experts(a):
                return a.rearrange("p (t o) -> p t o", o=1).to_broadcast([P, NT, E])

            def over_tiles(a, n_):
                return a.rearrange("p (o e) -> p o e", o=1).to_broadcast([P, n_, E])

            def picks():
                nonlocal route_count
                dve.wait_ge(logits_ready, GROUPS // 4)
                lg = logits[:, :, :]
                then(V.tensor_reduce(red[:, :], lg, axis=AX.X, op=ALU.max))
                then(V.tensor_tensor(prob2[:, :, :], lg, over_experts(red[:, :]), ALU.subtract))
                dve.wait_ge(exp_router, 1)
                then(V.tensor_reduce(red[:, :], prob[:, :, :], axis=AX.X, op=ALU.add))
                then(V.reciprocal(red[:, :], red[:, :]))
                then(V.tensor_tensor(prob[:, :, :], prob[:, :, :], over_experts(red[:, :]), ALU.mult))
                for c, pr in enumerate((prob, prob2)):
                    then(V.tensor_reduce(top[:, c, :], pr[:, :, :], axis=AX.X, op=ALU.max))
                    then(V.tensor_tensor(key[:, :, :], pr[:, :, :], over_experts(top[:, c, :]), ALU.is_equal))
                    then(V.tensor_tensor(key[:, :, :], key[:, :, :], over_tiles(order[:, :], NT), ALU.mult))
                    then(V.tensor_reduce(red[:, :], key[:, :, :], axis=AX.X, op=ALU.max))
                    then(V.tensor_tensor(pick[:, c, :, :], over_tiles(order[:, :], NT), over_experts(red[:, :]), ALU.is_equal))
                    if c == 0:
                        then(V.scalar_tensor_tensor(out=prob2[:, :, :].rearrange("p t e -> p (t e)"),
                                                    in0=pick[:, 0, :, :].rearrange("p t e -> p (t e)"), scalar=-2.0,
                                                    in1=prob[:, :, :].rearrange("p t e -> p (t e)"), op0=ALU.mult, op1=ALU.add))
                then(V.tensor_tensor(picked16[:, :, :], pick[:, 0, :, :], pick[:, 1, :, :], ALU.add))
                then(V.tensor_copy(record[:, :, :, 0].rearrange("p t c -> p c t"), top[:, :, :]))
                assert route_count == ROUTE_PICKED, route_count
            def places():
                nonlocal route_count
                dve.wait_ge(route_counts, 1)
                then(V.tensor_copy(total[:, :, :], wide[1][:, 512:1024].rearrange("p (t e) -> p t e", e=E)))
                for e in range(E):
                    V.tensor_tensor_scan(rank[:, :, e], ones[:, :], total[:, :, e], 0.0, ALU.mult, ALU.add).then_inc(route, 1)
                    route_count += 1
                dve.wait_ge(route, route_count)
                then(V.tensor_scalar(padded_i[:, :], rank[:, NT - 1, :], float(S - 1), None, ALU.add))
                then(V.tensor_scalar(padded_i[:, :], padded_i[:, :], S.bit_length() - 1, None, ALU.logical_shift_right))
                then(V.tensor_scalar(padded[:, :], padded_i[:, :], float(S), None, ALU.mult))
                then(V.tensor_tensor_scan(ends[:, :], ones[:, 0:E], padded[:, :], 0.0, ALU.mult, ALU.add))
                then(V.tensor_tensor(padded[:, :], ends[:, :], padded[:, :], ALU.subtract))
                then(V.tensor_tensor(rank[:, :, :], rank[:, :, :], total[:, :, :], ALU.subtract))
                then(V.tensor_tensor(rank[:, :, :], wide[1][:, 0:512].rearrange("p (t e) -> p t e", e=E), rank[:, :, :], ALU.add))
                then(V.tensor_tensor(rank[:, :, :], rank[:, :, :], over_tiles(padded[:, :], NT), ALU.add))
                for c in range(2):
                    then(V.tensor_tensor(key[:, :, :], pick[:, c, :, :], rank[:, :, :], ALU.mult))
                    then(V.tensor_reduce(slot[:, c, :], key[:, :, :], axis=AX.X, op=ALU.add))
                    then(V.tensor_copy(slot_i[:, :, c], slot[:, c, :]))
                then(V.tensor_tensor(past[:, :, :], tile_start[:, :].rearrange("p (t o) -> p t o", o=1).to_broadcast([P, NS, E]),
                                     over_tiles(ends[:, :], NS), ALU.is_ge))
                then(V.tensor_reduce(expert[:, :], past[:, :, :], axis=AX.X, op=ALU.add))
                then(V.tensor_scalar(padded_experts[:, 2:2 + NS], expert[:, :], float(E - 1), None, ALU.min))
                for j in range(FIELDS):
                    u, place = divmod(j, FIELDS // 2)
                    field = padded_experts[:, j:j + UNROLL * (RUNS - 1) + 1:UNROLL]
                    if place == 0:
                        then(V.tensor_copy(packed[:, u, :], field))
                    else:
                        then(V.scalar_tensor_tensor(out=packed[:, u, :], in0=field, scalar=float(1 << BITS * place), in1=packed[:, u, :],
                                                    op0=ALU.mult, op1=ALU.add))
                then(V.tensor_copy(packed_i[:, :, :], packed[:, :, :]))
                then(V.tensor_scalar(packed_i[:, 1, :], packed_i[:, 1, :], BITS * FIELDS // 2, None, ALU.logical_shift_left))
                then(V.tensor_tensor(packed_i[:, 0, :], packed_i[:, 0, :], packed_i[:, 1, :], ALU.bitwise_or))
                assert route_count == ROUTE_DONE, route_count

            def maximum(s, m):
                ps, empty = full(dve, s, f"m{m}")
                g, u = divmod(m, 3)
                if u == 0:
                    dst, nh = shift[:, 0, :, g], 4
                else:
                    dst, nh = shift[:, 1, 2 * (u - 1):2 * u, g], 2
                V.tensor_reduce(dst, ps[:, :].rearrange("p (j k) -> p j k", j=nh), axis=AX.X, op=ALU.max,
                                negate=True).then_inc(empty, 1)

            def normalise(s, t):
                ps, empty = full(dve, s, f"oT{t}")
                heads = ps[:, :].rearrange("p (h r) -> p h r", r=ROWS)
                V.reciprocal(rden[:, :], heads[:, :, HD]).then_inc(rden_ready, 1)
                dve.wait_ge(rden_ready, (s - FINISH) * 2 + (t + 1))
                V.tensor_tensor(o_n[:, t, :, :], heads[:, :, 0:HD],
                                rden[:, :].rearrange("p (h o) -> p h o", o=1).to_broadcast([P, H, HD]), ALU.mult).then_inc(empty, 1)

            def low_parts(s):
                ps, empty = full(dve, s, "qk")
                dve.wait_ge(qk_hi_ready, s + 1)
                V.tensor_tensor(split[:, 2:6:3, :], ps[:, :].rearrange("p (c q) -> p c q", c=2),
                                split[:, 0:5:4, :], ALU.subtract).then_inc(empty, 1)
                V.tensor_copy(split[:, 1:7:5, :], split[:, 0:5:4, :]).then_inc(qk_high_ready, 1)

            def add_and_measure(s):
                b = s - FINISH
                ps, empty = full(dve, s, "proj")
                dve.wait_ge(xpb_ready, b * 1 + 1)
                V.tensor_tensor(x2[:, :, :], ps[:, 0:QT * D].rearrange("p (t d) -> p t d", t=QT), xpb[:, :, :], ALU.add).then_inc(empty, 1)
                made(dve, s, "proj")
                for t in range(QT):
                    V.bn_stats(st2[:, t, :], x2[:, t, :]).then_inc(st2_ready, 1)
                dve.wait_ge(st2_ready, b * 2 + 2)
                dve.nop(nofuse=True)
                for t in range(QT):
                    V.bn_aggr(mv2[:, t, :], st2[:, t, :]).then_inc(mv2_ready, 1)
                dve.wait_ge(mv2_ready, b * 3 + 2)
                V.tensor_scalar(mv2[:, :, 1], mv2[:, :, 1], LN_EPS, None, ALU.add).then_inc(mv2_ready, 1)

            def last(s):
                b = s - LAST
                for t in range(QT):
                    V.scalar_tensor_tensor(out=y2[:, t, :], in0=x2[:, t, :], scalar=mv2[:, t, 0:1], in1=gamma_bc[:, :],
                                           op0=ALU.subtract, op1=ALU.mult).then_inc(y2_ready, 1)
                dve.wait_ge(rstd2_ready, b * 1 + 1)
                dve.wait_ge(offset_ready, b * 1 + 1)
                for t in range(QT):
                    dve.wait_ge(y2_ready, b * 2 + (t + 1))
                    mine = x_all[:, bass.ds(b * QT + t, 1), :].rearrange("p a d -> p (a d)")
                    V.scalar_tensor_tensor(out=mine, in0=y2[:, t, :], scalar=rstd2[:, t:t + 1], in1=mine,
                                           op0=ALU.mult, op1=ALU.add).then_inc(res_ready, 1)

            def step(s, par):
                for _, what, stage_ in USES:
                    if not has(s, stage_):
                        pass
                    elif what[0] == "m":
                        maximum(s, int(what[1:]))
                    elif what == "qk":
                        low_parts(s)
                    elif what[:2] == "oT":
                        normalise(s, int(what[2:]))
                    elif what == "proj":
                        add_and_measure(s)
                    if what == LAST_AFTER and has(s, LAST):
                        last(s)
                for i in pieces(s):
                    dve.wait_ge(piece_high, i + 1)
                    V.tensor_tensor(part_of(i, 1), piece[i % 2], part_of(i, 0), ALU.subtract).then_inc(piece_low, 1)

            steps(dve, step, after=((picks,), (places,)))
            dve.wait_ge(expert_weights, 32)
            V.tensor_copy(b2_high[:, :, :], b2_twice[:, :, :]).then_inc(b2_ready, 1)
            dve.wait_ge(b2_ready, 1)
            V.scalar_tensor_tensor(out=b2_parts[:, :, :], in0=b2_high[:, :, :], scalar=minus_row[:, :], in1=b2_twice[:, :, :],
                                   op0=ALU.mult, op1=ALU.add).then_inc(b2_ready, 1)

            def low_hidden(s, par, half_):
                cs = slice(HC // 2 * half_, HC // 2 * (half_ + 1))
                if half_ == 0:
                    dve.wait_ge(h_high, s + 1)
                else:
                    dve.wait_ge(h_ready, s * HC + HC)
                    V.tensor_copy(hT_parts[:, par, 0, cs, :], hT[:, par, cs, :]).then_inc(h_high_2, 1)
                    dve.wait_ge(h_high_2, s + 1)
                V.tensor_tensor(hT_parts[:, par, 1, cs, :], hT[:, par, cs, :], hT_parts[:, par, 0, cs, :],
                                ALU.subtract).then_inc(h_parts_ready, 1)

            def tile(s, k, experts):
                quad = k % 4
                par = quad % 2
                if first(s):
                    dve.wait_ge(xg_loaded[quad], (s - quad) * 4 + 16)
                    later(dve, placed[quad], (s - quad) * 8, beyond(s, 3))
                    V.tensor_tensor(dest[:, quad, :], xg[:, quad, :, D + 1].bitcast(I32), spare_row[:, bass.ds(s * 2, 2)], ALU.min).then_inc(xg_used, 1)
                    dve.wait_ge(xg_T_high, s + 1)
                    V.tensor_tensor(xgT[:, par, 1, :], bank[("misc", "maxA")[par]][:, 0:S], xgT[:, par, 0, :], ALU.subtract).then_inc(xg_T_ready, 1)
                    V.tensor_copy(weight[:, quad, :], xg[:, quad, :, D]).then_inc(xg_used, 1)
                if hides(s):
                    low_hidden(s - 1, 1 - par, 0)
                    low_hidden(s - 1, 1 - par, 1)

            tiles(dve, tile, load=False)
            for c in range(LAST_CHUNKS):
                mine = parts[:, c % PART_BUFS, :, :]
                here = x_all[:, LC * c:LC * (c + 1), :]
                dve.wait_ge(parts_loaded[c % PART_BUFS], 16 * (c // PART_BUFS + 1))
                V.tensor_tensor(mine[:, :, 0:D], mine[:, :, 0:D], mine[:, :, D:2 * D], ALU.add).then_inc(parts_added, 1)
                dve.wait_ge(parts_added, c + 1)
                V.tensor_tensor(here, here, mine[:, :, 0:D], ALU.add).then_inc(out_ready, 1)

        @block.tensor
        def _(pe):
            M = nc.tensor.matmul
            pe.wait_ge(weights_loaded, 96)
            pe.wait_ge(consts, 23)
            nc.tensor.transpose(bank["head"][:, 0:E], wr[:, :], ident[0:E, 0:E]).then_inc(wrT_filled, 1)
            pe.wait_ge(wrT_ready, 1)

            def router(g, q, b):
                pe.wait_ge(xnT_ready, g * 2 + 1)
                if q == 0:
                    later(pe, lgT_ready, b, beyond(b, 0))
                for u in range(4):
                    last = M(bank["misc"][32 * u:32 * (u + 1), P * q:P * (q + 1)], wrT[:, :],
                             stage_T[:, q % 2, P * u:P * (u + 1)], start=True, stop=True, skip_group_check=True)
                if q == 3:
                    last.then_inc(lgT_filled, 1)

            def by_token(b):
                pe.wait_ge(lgT_ready, b + 1)
                later(pe, logits_ready, b, beyond(b, 0))
                for q in range(4):
                    last = nc.tensor.transpose(bank["head"][:, P * q:P * (q + 1)], lgT[:, P * q:P * (q + 1)], ident[:, :])
                last.then_inc(logits_filled, 1)

            def group(g, q, b):
                pe.wait_ge(staged, g + 1)
                later(pe, xnT_ready, g * 2 - 2, beyond(g, 1))
                ps = bank[("maxA", "maxB")[q % 2]]
                for u in range(4):
                    last = nc.tensor.transpose(ps[:, P * u:P * (u + 1)], stage[:, q % 2, u, :], ident[:, :])
                last.then_inc(xnT_filled, 1)
                if q > 0:
                    router(g - 1, q - 1, b)
                elif beyond(b, 0):
                    router(g - 1, 3, b - 1)
                if q == 1 and beyond(b, 0):
                    by_token(b - 1)

            groups(pe, group)
            router(GROUPS - 1, 3, GROUPS // 4 - 1)
            by_token(GROUPS // 4 - 1)
            pe.wait_ge(logits_ready, GROUPS // 4)

            def count_picks():
                pe.wait_ge(route, ROUTE_PICKED)
                flat = picked16[:, :, :].rearrange("p t e -> p (t e)")
                M(wide[1][:, 0:512], before16[:, :], flat, start=True, stop=True)
                M(wide[1][:, 512:1024], ones16[:, :], flat, start=True, stop=True).then_inc(route_counts, 1)

            def step(s, par):
                b = s - SOFT

                def scores(u):
                    ps, fill_ = room(pe, s, f"s{u}")
                    kt, gs = SCORES[u]
                    keys = k_cat[:, par, :, P * kt:P * (kt + 1)]
                    if kt == 0:
                        for h2 in range(2):
                            last = M(ps[:, 512 * h2:512 * (h2 + 1)], keys[:, gs[0], :],
                                     q_diag[:, par, gs[0], 2 * h2:2 * h2 + 2, :], start=True, stop=True)
                    else:
                        for n_, g in enumerate(gs):
                            last = M(ps[:, 512 * n_:512 * (n_ + 1)], keys[:, g, :],
                                     q_diag[:, par, g, :, P:T], start=True, stop=True)
                    last.then_inc(fill_, 1)

                def maxima(m):
                    ps, fill_ = room(pe, s, f"m{m}")
                    g, u = divmod(m, 3)
                    qt, js, keys = (0, range(J), P) if u == 0 else (1, (2 * u - 2, 2 * u - 1), T)
                    for n_, j in enumerate(js):
                        M(ps[:, keys * n_:keys * (n_ + 1)], q_diag[:, 1 - par, g, j, P * qt:P * (qt + 1)],
                          k_cat[:, 1 - par, g, 0:keys], start=(n_ == 0), stop=False, skip_group_check=True)
                    nh = len(js)
                    dst = ps[:, :].rearrange("p (j k) -> p j k", j=nh)[:, :, keys - P:keys]
                    M(dst, ident16[:, :], mask16[:, :].rearrange("p (o k) -> p o k", o=1).to_broadcast([P, nh, P]),
                      start=False, stop=True, skip_group_check=True).then_inc(fill_, 1)

                def values(half_, of, count):
                    ps, fill_ = room(pe, s, f"o{half_}")
                    first_ = 3 * half_
                    pe.wait_ge(probs_ready, count)
                    for n_ in range(2):
                        g = 2 * half_ + n_
                        for kt in range(QT):
                            for j in range(J):
                                if kt == 0:
                                    p_, dst = probs[:, first_ + n_, T * j:T * (j + 1)], ps[32 * j:32 * (j + 1), T * n_:T * (n_ + 1)]
                                else:
                                    at = 512 * n_ + P * j
                                    p_, dst = probs[:, first_ + 2, at:at + P], ps[32 * j:32 * (j + 1), T * n_ + P:T * (n_ + 1)]
                                last = M(dst, v_aug[:, of, kt, J * g + j, :], p_, start=(kt == 0), stop=(kt == 1),
                                         skip_group_check=True)
                    last.then_inc(fill_, 1)

                def project_qk():
                    ps, fill_ = room(pe, s, "qk")
                    for c in range(2):
                        last = M(ps[:, T * c:T * (c + 1)], wqkv[:, D * c:D * (c + 1)], xnT_all[:, bass.ds(s * T, T)], start=True, stop=True)
                    last.then_inc(fill_, 1)

                def project_v():
                    pe.wait_ge(xbT_ready, s * 1)
                    ps, fill_ = room(pe, s, "v")
                    for t in range(QT):
                        last = M(ps[:, D * t:D * (t + 1)], xbT[:, 1 - par, P * t:P * (t + 1)], wqkv[:, 2 * D:3 * D], start=True, stop=True)
                    last.then_inc(fill_, 1)

                def transpose_sums(t):
                    ps, fill_ = room(pe, s, f"oT{t}")
                    if t == 0:
                        made(pe, s, "o1")
                    for g in range(G):
                        last = nc.tensor.transpose(ps[:, P * g:P * (g + 1)], o_T[:, g, P * t:P * (t + 1)], ident[:, :])
                    last.then_inc(fill_, 1)

                def transpose_shifts():
                    made(pe, s, "m10")
                    made(pe, s, "m11")
                    ps, fill_ = room(pe, s, "shift")
                    for t in range(QT):
                        last = nc.tensor.transpose(ps[0:H, P * t:P * (t + 1)],
                                                   shift[:, t, :, :].rearrange("p j g -> p (j g)"), ident[:, :])
                    last.then_inc(fill_, 1)

                def transpose_normed():
                    made(pe, s, "oT1")
                    ps, fill_ = room(pe, s, "onT")
                    for t in range(QT):
                        last = nc.tensor.transpose(ps[:, P * t:P * (t + 1)], o_n[:, t, :, :].rearrange("p h d -> p (h d)"), ident[:, :])
                    last.then_inc(fill_, 1)

                def project_out():
                    made(pe, s, "onT")
                    ps, fill_ = room(pe, s, "proj")
                    for t in range(QT):
                        last = M(ps[:, D * t:D * (t + 1)], o_nT[:, P * t:P * (t + 1)], wp[:, :], start=True, stop=True)
                    last.then_inc(fill_, 1)

                for _, what, stage_ in USES:
                    if not has(s, stage_):
                        continue
                    if what == "o1":
                        values(1, 1 - par, (s - FINISH) * 6 + 6)
                    elif what == "o0":
                        made(pe, s - 1, "v")
                        values(0, par, b * 6 + 3)
                    elif what[0] == "m":
                        if what in ("m0", "m6"):
                            pe.wait_ge(half_loaded[what == "m6"], (s - MAXIMA) * 80 + 80)
                        maxima(int(what[1:]))
                    elif what[0] == "s" and what != "shift":
                        if what == "s0":
                            if isinstance(s, int) and s == SOFT:
                                pe.wait_ge(route, ROUTE_DONE)
                            pe.wait_ge(shift_loaded, b * (16 * J) + 16 * J)
                        scores(int(what[1:]))
                    elif what[:2] == "oT":
                        transpose_sums(int(what[2:]))
                    else:
                        {"qk": project_qk, "v": project_v, "shift": transpose_shifts,
                         "onT": transpose_normed, "proj": project_out}[what]()

            steps(pe, step, after=((), (count_picks,)))
            for name in filled:
                pe.wait_ge(emptied[name], B * sum(n == name for n, _, _ in USES))
            pe.wait_ge(piece_low, PIECES)
            pe.wait_ge(b2_ready, 2)
            PRODUCTS = ((0, 0), (0, 1), (1, 0))

            def tile(s, k, experts):
                quad = k % 4
                par = quad % 2
                e_2, e_1 = expert_of(experts, k, 2), expert_of(experts, k, 0)
                if first(s):
                    pe.wait_ge(xg_loaded[quad], (s - quad) * 4 + 16)
                    later(pe, xg_T_ready, s - 1, beyond(s, 1))
                    for t in range(2):
                        last = nc.tensor.transpose(bank[("misc", "maxA")[par]][:, P * t:P * (t + 1)], xg[:, quad, t, 0:D], ident[:, :])
                    last.then_inc(xg_T_filled, 1)
                if second(s):
                    later(pe, y_ready, s * 2 - 6, beyond(s, 3))
                    results = bank[("head", "maxB")[par]]
                    for t in range(2):
                        M(results[:, D * t:D * (t + 1)], one_rows[:, :], b2_parts[:, bass.ds(e_2, 1), :].rearrange("p a d -> p (a d)"),
                          start=(t == 0), stop=False, skip_group_check=True)
                    for c in range(HC):
                        if c % 2 == 0:
                            pe.wait_ge(h_parts_ready, s * 2 + (c // 2 - 3))
                        for t in range(2):
                            for n_, (hp, wp_) in enumerate(PRODUCTS):
                                last = M(results[:, D * t:D * (t + 1)], hT_parts[:, par, hp, c, P * t:P * (t + 1)],
                                         w2_parts[:, wp_, bass.ds(e_2, 1), c, :].rearrange("p a d -> p (a d)"),
                                         start=False, stop=(c == HC - 1 and n_ == 2), skip_group_check=True)
                    last.then_inc(y_filled, 1)
                if first(s):
                    pe.wait_ge(xg_T_ready, s + 1)
                    for c in range(HC):
                        for n_, (wp_, xp) in enumerate(PRODUCTS):
                            last = M(wide[par][:, S * c:S * (c + 1)], w1_parts[:, wp_, bass.ds(e_1, 1), P * c:P * (c + 1)].rearrange("p a d -> p (a d)"),
                                     xgT[:, par, xp, :], start=(n_ == 0), stop=(n_ == 2))
                        if c % 2 == 1:
                            last.then_inc(h_filled, 1)

            tiles(pe, tile)


_INS = {
    "L0_attn_target": "x", "L0_attn_w_qkv": "w_qkv", "L0_attn_w_proj": "w_proj", "L0_attn_b_proj": "b_proj",
    "L0_attn_ln_gamma": "gamma", "L0_attn_ln_beta": "beta", "L0_ffn_Wr": "w_router",
    "L0_ffn_W1": "w1", "L0_ffn_b1": "b1", "L0_ffn_W2": "w2", "L0_ffn_b2": "b2",
}


def kernel(**inputs):
    import numpy as np
    from concourse import bacc
    from concourse.bass_utils import run_bass_kernel_spmd

    nc = bacc.Bacc("TRN2", target_bir_lowering=False, num_devices=1)
    arrays, args = {}, {}
    for name, short in _INS.items():
        a = np.ascontiguousarray(inputs[name])
        arrays[f"in_{short}"] = a
        args[short] = nc.dram_tensor(f"in_{short}", a.shape, mybir.dt.from_np(a.dtype), kind="ExternalInput").ap()
    out = nc.dram_tensor("out_0", inputs["L0_attn_target"].shape, F32, kind="ExternalOutput").ap()
    attention_and_moe(nc, out=out, **args)
    r = run_bass_kernel_spmd(nc, [arrays], core_ids=[0])
    return r.results[0]["out_0"]
```
